# Optimizing a Trainium2 kernel written in Bass

```python
import numpy as np
import jax
import jax.numpy as jnp

def _softmax(x, axis=-1):
    return jax.nn.softmax(x, axis=axis)

def _gelu(x):
    return jax.nn.gelu(x, approximate=True)

def _silu(x):
    return jax.nn.silu(x)

def _sigmoid(x):
    return jax.nn.sigmoid(x)

def _layernorm(x, axis=-1, eps=1e-05):
    m = jnp.mean(x, axis=axis, keepdims=True)
    v = jnp.var(x, axis=axis, keepdims=True)
    return (x - m) / jnp.sqrt(v + eps)

def _scatter_add(tgt, idx, src, axis=0):
    return tgt.at[idx].add(src)

def _segment_sum(src, seg, n):
    return jax.ops.segment_sum(src, seg, n)
kernel_name = 'mk_sandwich_d1_jaxref_r8_1535c7'

def setup_inputs(seed: int=0):
    np.random.seed(seed)
    _w = jnp.asarray

    def _L0_attn_setup():
        import jax, jax.numpy as jnp
        import numpy as np
        EPS = 1e-06
        ROPE_BASE = 10000.0

        def _rmsnorm(x, w):
            var = jnp.mean(x * x, axis=-1, keepdims=True)
            return x * jax.lax.rsqrt(var + EPS) * w

        def _rope(t):
            S, D = (t.shape[-2], t.shape[-1])
            inv_freq = 1.0 / ROPE_BASE ** (jnp.arange(0, D, 2, dtype=jnp.float32) / D)
            ang = jnp.arange(S, dtype=jnp.float32)[:, None] * inv_freq
            cos = jnp.concatenate([jnp.cos(ang), jnp.cos(ang)], axis=-1)
            sin = jnp.concatenate([jnp.sin(ang), jnp.sin(ang)], axis=-1)
            t1, t2 = jnp.split(t, 2, axis=-1)
            rot = jnp.concatenate([-t2, t1], axis=-1)
            return t * cos + rot * sin
        key = jax.random.key(seed)
        ks = jax.random.split(key, 9)
        B, S, H = (2, 256, 256)
        Hq, Hkv, D = (16, 4, 128)
        s = 0.02
        return {'x': jax.random.normal(ks[0], (B, S, H), jnp.float32), 'q_project': jax.random.normal(ks[1], (Hq * D, H), jnp.float32) * s, 'k_project': jax.random.normal(ks[2], (Hkv * D, H), jnp.float32) * s, 'v_project': jax.random.normal(ks[3], (Hkv * D, H), jnp.float32) * s, 'q_bias': jax.random.normal(ks[4], (Hq * D,), jnp.float32) * s, 'k_bias': jax.random.normal(ks[5], (Hkv * D,), jnp.float32) * s, 'v_bias': jax.random.normal(ks[6], (Hkv * D,), jnp.float32) * s, 'o_project': jax.random.normal(ks[7], (H, Hq * D), jnp.float32) * s, 'ln_weight': jnp.ones((H,), jnp.float32)}
    _L0_attn_in = _L0_attn_setup()

    def _L0_ffn_setup():
        import jax, jax.numpy as jnp
        import numpy as np
        B, S, H = (1, 128, 256)
        NH, NKV, D = (32, 8, 64)
        GROUPS = NH // NKV
        E, F, TOPK = (8, 1024, 2)
        EPS = 1e-05

        def rmsnorm(x, w):
            return x * jax.lax.rsqrt(jnp.mean(x * x, axis=-1, keepdims=True) + EPS) * w

        def attention(h, wq, wk, wv, wo):
            b, s, _ = h.shape
            q = (h @ wq).reshape(b, s, NH, D).transpose(0, 2, 1, 3)
            k = (h @ wk).reshape(b, s, NKV, D).transpose(0, 2, 1, 3)
            v = (h @ wv).reshape(b, s, NKV, D).transpose(0, 2, 1, 3)
            k = jnp.repeat(k, GROUPS, axis=1)
            v = jnp.repeat(v, GROUPS, axis=1)
            scores = jnp.einsum('bhqd,bhkd->bhqk', q, k) / jnp.sqrt(jnp.float32(D))
            causal = jnp.tril(jnp.ones((s, s), bool))
            scores = jnp.where(causal, scores, jnp.finfo(scores.dtype).min)
            attn = jax.nn.softmax(scores, axis=-1)
            out = jnp.einsum('bhqk,bhkd->bhqd', attn, v)
            out = out.transpose(0, 2, 1, 3).reshape(b, s, NH * D)
            return out @ wo

        def moe(h, gate_w, w1, w2, w3):
            b, s, hd = h.shape
            t = h.reshape(-1, hd)
            T = t.shape[0]
            probs = jax.nn.softmax(t @ gate_w, axis=-1)
            topw, topi = jax.lax.top_k(probs, TOPK)
            topw = topw / jnp.sum(topw, axis=-1, keepdims=True)
            combine = jnp.zeros((T, E), t.dtype).at[jnp.arange(T)[:, None], topi].add(topw)
            up = jnp.einsum('th,ehf->etf', t, w1)
            gated = jax.nn.relu(up) * jnp.einsum('th,ehf->etf', t, w3)
            down = jnp.einsum('etf,efh->eth', gated, w2)
            out = jnp.einsum('eth,te->th', down, combine)
            return out.reshape(b, s, hd)
        key = jax.random.key(seed)
        ks = jax.random.split(key, 12)
        sc = 0.02
        return {'x': jax.random.normal(ks[0], (B, S, H), dtype=jnp.float32), 'ln1_w': jnp.ones((H,), jnp.float32), 'wq': jax.random.normal(ks[1], (H, NH * D), jnp.float32) * sc, 'wk': jax.random.normal(ks[2], (H, NKV * D), jnp.float32) * sc, 'wv': jax.random.normal(ks[3], (H, NKV * D), jnp.float32) * sc, 'wo': jax.random.normal(ks[4], (NH * D, H), jnp.float32) * sc, 'ln2_w': jnp.ones((H,), jnp.float32), 'gate_w': jax.random.normal(ks[5], (H, E), jnp.float32) * sc, 'w1': jax.random.normal(ks[6], (E, H, F), jnp.float32) * sc, 'w2': jax.random.normal(ks[7], (E, F, H), jnp.float32) * sc, 'w3': jax.random.normal(ks[8], (E, H, F), jnp.float32) * sc}
    _L0_ffn_in = _L0_ffn_setup()
    _d = {'L0_attn_x': _L0_attn_in['x'], 'L0_attn_q_project': _L0_attn_in['q_project'], 'L0_attn_k_project': _L0_attn_in['k_project'], 'L0_attn_v_project': _L0_attn_in['v_project'], 'L0_attn_q_bias': _L0_attn_in['q_bias'], 'L0_attn_k_bias': _L0_attn_in['k_bias'], 'L0_attn_v_bias': _L0_attn_in['v_bias'], 'L0_attn_o_project': _L0_attn_in['o_project'], 'L0_attn_ln_weight': _L0_attn_in['ln_weight'], 'L0_ffn_ln1_w': _L0_ffn_in['ln1_w'], 'L0_ffn_wq': _L0_ffn_in['wq'], 'L0_ffn_wk': _L0_ffn_in['wk'], 'L0_ffn_wv': _L0_ffn_in['wv'], 'L0_ffn_wo': _L0_ffn_in['wo'], 'L0_ffn_ln2_w': _L0_ffn_in['ln2_w'], 'L0_ffn_gate_w': _L0_ffn_in['gate_w'], 'L0_ffn_w1': _L0_ffn_in['w1'], 'L0_ffn_w2': _L0_ffn_in['w2'], 'L0_ffn_w3': _L0_ffn_in['w3']}
    _x0 = _d['L0_attn_x']
    _d['L0_attn_x'] = jax.random.normal(jax.random.fold_in(jax.random.key(seed), 1), (4, 512, 256), dtype=_x0.dtype)
    del _x0
    return _d

def reference(L0_attn_x, L0_attn_q_project, L0_attn_k_project, L0_attn_v_project, L0_attn_q_bias, L0_attn_k_bias, L0_attn_v_bias, L0_attn_o_project, L0_attn_ln_weight, L0_ffn_ln1_w, L0_ffn_wq, L0_ffn_wk, L0_ffn_wv, L0_ffn_wo, L0_ffn_ln2_w, L0_ffn_gate_w, L0_ffn_w1, L0_ffn_w2, L0_ffn_w3):

    def _L0_attn_ref(x, q_project, k_project, v_project, q_bias, k_bias, v_bias, o_project, ln_weight):
        import jax, jax.numpy as jnp
        import numpy as np
        EPS = 1e-06
        ROPE_BASE = 10000.0

        def _rmsnorm(x, w):
            var = jnp.mean(x * x, axis=-1, keepdims=True)
            return x * jax.lax.rsqrt(var + EPS) * w

        def _rope(t):
            S, D = (t.shape[-2], t.shape[-1])
            inv_freq = 1.0 / ROPE_BASE ** (jnp.arange(0, D, 2, dtype=jnp.float32) / D)
            ang = jnp.arange(S, dtype=jnp.float32)[:, None] * inv_freq
            cos = jnp.concatenate([jnp.cos(ang), jnp.cos(ang)], axis=-1)
            sin = jnp.concatenate([jnp.sin(ang), jnp.sin(ang)], axis=-1)
            t1, t2 = jnp.split(t, 2, axis=-1)
            rot = jnp.concatenate([-t2, t1], axis=-1)
            return t * cos + rot * sin
        B, S, _ = x.shape
        Hq, Hkv, D = (16, 4, 128)
        rep = Hq // Hkv
        h = _rmsnorm(x, ln_weight)
        q = h @ q_project.T + q_bias
        k = h @ k_project.T + k_bias
        v = h @ v_project.T + v_bias
        q = q.reshape(B, S, Hq, D).transpose(0, 2, 1, 3)
        k = k.reshape(B, S, Hkv, D).transpose(0, 2, 1, 3)
        v = v.reshape(B, S, Hkv, D).transpose(0, 2, 1, 3)
        q = _rope(q)
        k = _rope(k)
        qg = q.reshape(B, Hkv, rep, S, D)
        scale = jnp.float32(1.0) / jnp.sqrt(jnp.float32(D))
        scores = jnp.einsum('bgrqd,bgkd->bgrqk', qg, k) * scale
        mask = jnp.where(jnp.tril(jnp.ones((S, S), bool)), 0.0, -jnp.inf).astype(scores.dtype)
        attn = jax.nn.softmax(scores + mask, axis=-1)
        out = jnp.einsum('bgrqk,bgkd->bgrqd', attn, v)
        out = out.reshape(B, Hq, S, D).transpose(0, 2, 1, 3).reshape(B, S, Hq * D)
        return out @ o_project.T

    def _L0_ffn_ref(x, ln1_w, wq, wk, wv, wo, ln2_w, gate_w, w1, w2, w3):
        import jax, jax.numpy as jnp
        import numpy as np
        B, S, H = (1, 128, 256)
        NH, NKV, D = (32, 8, 64)
        GROUPS = NH // NKV
        E, F, TOPK = (8, 1024, 2)
        EPS = 1e-05

        def rmsnorm(x, w):
            return x * jax.lax.rsqrt(jnp.mean(x * x, axis=-1, keepdims=True) + EPS) * w

        def attention(h, wq, wk, wv, wo):
            b, s, _ = h.shape
            q = (h @ wq).reshape(b, s, NH, D).transpose(0, 2, 1, 3)
            k = (h @ wk).reshape(b, s, NKV, D).transpose(0, 2, 1, 3)
            v = (h @ wv).reshape(b, s, NKV, D).transpose(0, 2, 1, 3)
            k = jnp.repeat(k, GROUPS, axis=1)
            v = jnp.repeat(v, GROUPS, axis=1)
            scores = jnp.einsum('bhqd,bhkd->bhqk', q, k) / jnp.sqrt(jnp.float32(D))
            causal = jnp.tril(jnp.ones((s, s), bool))
            scores = jnp.where(causal, scores, jnp.finfo(scores.dtype).min)
            attn = jax.nn.softmax(scores, axis=-1)
            out = jnp.einsum('bhqk,bhkd->bhqd', attn, v)
            out = out.transpose(0, 2, 1, 3).reshape(b, s, NH * D)
            return out @ wo

        def moe(h, gate_w, w1, w2, w3):
            b, s, hd = h.shape
            t = h.reshape(-1, hd)
            T = t.shape[0]
            probs = jax.nn.softmax(t @ gate_w, axis=-1)
            topw, topi = jax.lax.top_k(probs, TOPK)
            topw = topw / jnp.sum(topw, axis=-1, keepdims=True)
            combine = jnp.zeros((T, E), t.dtype).at[jnp.arange(T)[:, None], topi].add(topw)
            up = jnp.einsum('th,ehf->etf', t, w1)
            gated = jax.nn.relu(up) * jnp.einsum('th,ehf->etf', t, w3)
            down = jnp.einsum('etf,efh->eth', gated, w2)
            out = jnp.einsum('eth,te->th', down, combine)
            return out.reshape(b, s, hd)
        h = x + attention(rmsnorm(x, ln1_w), wq, wk, wv, wo)
        return h + moe(rmsnorm(h, ln2_w), gate_w, w1, w2, w3)
    x = L0_attn_x
    x = x + _layernorm(_L0_attn_ref(_layernorm(x, axis=-1), L0_attn_q_project, L0_attn_k_project, L0_attn_v_project, L0_attn_q_bias, L0_attn_k_bias, L0_attn_v_bias, L0_attn_o_project, L0_attn_ln_weight), axis=-1)
    x = x + _layernorm(_L0_ffn_ref(_layernorm(x, axis=-1), L0_ffn_ln1_w, L0_ffn_wq, L0_ffn_wk, L0_ffn_wv, L0_ffn_wo, L0_ffn_ln2_w, L0_ffn_gate_w, L0_ffn_w1, L0_ffn_w2, L0_ffn_w3), axis=-1)
    return x

_drawn_inputs = setup_inputs


def setup_inputs(seed=0):
    import zlib

    import numpy as np

    out = dict(_drawn_inputs(seed))
    spreads = {'L0_attn_ln_weight': (1.0, 0.2), 'L0_ffn_ln1_w': (1.0, 0.6), 'L0_ffn_ln2_w': (1.0, 0.6)}
    factors = {'L0_attn_q_bias': 8.0,
     'L0_attn_k_bias': 8.0,
     'L0_ffn_wq': 8.0,
     'L0_ffn_wk': 8.0,
     'L0_ffn_gate_w': 4.278,
     'L0_ffn_w1': 4.473,
     'L0_ffn_w2': 3.744,
     'L0_ffn_w3': 3.78}
    for name, (base, spread) in spreads.items():
        noise = np.random.default_rng([zlib.crc32(name.encode()), seed]).standard_normal(out[name].shape)
        drawn = base * np.exp(spread * noise) if base else spread * noise
        out[name] = jnp.asarray(drawn.astype(out[name].dtype))
    for name, factor in factors.items():
        out[name] = (out[name] * factor).astype(out[name].dtype)
    return out
```

```python
from contextlib import ExitStack

import concourse.bass as bass
from concourse import mybir

F32 = mybir.dt.float32
F32R = mybir.dt.float32r
BF16 = mybir.dt.bfloat16
I32 = mybir.dt.int32
U32 = mybir.dt.uint32
ALU = mybir.AluOpType
ACT = mybir.ActivationFunctionType
AX_X = mybir.AxisListType.X

P = 128
B, S, H = 4, 512, 256
T = B * S
TILES = T // P
KT = H // P
QT = S // P
G = 4
QROWS = 512
QTILES = QROWS // P
WROWS = QROWS + 2 * P
PROJ = WROWS // P
T_K, T_V = QTILES, QTILES + 1
STEPS = B * G
D1, D2 = 128, 64
E, F = 8, 1024
FT = F // P
TB = T // 512
LN_EPS = 1e-5
RMS_A_EPS = 1e-6
RMS_B_EPS = 1e-5
MASKED = -1e30
LAG = 3
N_SCORE = 4
N_PROB = 4
N_TURN = 2
N_GATED = 4


def program(nc, x_in, cos_in, sin_in, wa_in, ba_in, oa_in,
            wb_in, ob_in, ln_in, gate_in, w1_in, w2_in, w3_in, out):
    with ExitStack() as ctx:
        def sb(name, shape, dt=F32, stack=ctx):
            return stack.enter_context(nc.sbuf_tensor(name, shape, dt))

        def sem(name):
            return ctx.enter_context(nc.semaphore(name))

        bank = [ctx.enter_context(nc.psum_tensor(f"bank{i}", [P, 512], F32)) for i in range(8)]
        score_bank, turn_bank, o_bank, x_bank = bank[0:4], bank[4:6], bank[6], bank[7]
        up_bank, lin_bank, down_bank, logit_bank = bank[0:2], bank[2:4], bank[4:6], bank[6]

        x = sb("x", [P, TILES, H])
        acc = sb("acc", [P, TILES, H])
        htok = sb("htok", [P, TILES, H])
        hT = sb("hT", [P, KT, T])
        identity = sb("identity", [P, P])
        causal = sb("causal", [P, P])
        identity_b = sb("identity_b", [P, P], BF16)
        causal_b = sb("causal_b", [P, P], BF16)
        iota_i = sb("iota_i", [P, TILES, E], I32)
        iota_e = sb("iota_e", [P, TILES, E])
        ln_w = sb("ln_w", [P, 3, KT])
        gate_w = sb("gate_w", [P, KT, E])
        stats = sb("stats", [P, TILES, 6])
        mv = sb("mv", [P, TILES, 2])
        square = sb("square", [P, TILES])
        root = sb("root", [P, TILES])
        inv1 = sb("inv1", [P, TILES])
        inv2 = sb("inv2", [P, TILES])
        scale = sb("scale", [P, TILES])
        shift = sb("shift", [P, TILES])
        e_max = sb("e_max", [P, TILES])
        e_sum = sb("e_sum", [P, TILES])
        e_prob = sb("e_prob", [P, TILES, E])
        e_top = sb("e_top", [P, TILES, E])
        e_topi = sb("e_topi", [P, TILES, E], U32)
        e_topf = sb("e_topf", [P, TILES, E])
        pick = sb("pick", [P, TILES, E])
        combine = sb("combine", [P, TILES, E])

        both, first_only, second_only = ExitStack(), ExitStack(), ExitStack()
        cosT = sb("cosT", [P, S], stack=first_only)
        sinT = sb("sinT", [P, S], stack=first_only)
        unroped = sb("unroped", [P, 2, S], stack=first_only)
        times_cos = sb("times_cos", [P, 2, S], stack=first_only)
        times_sin = sb("times_sin", [P, 2, S], stack=first_only)
        qT = sb("qT", [P, QTILES, S], stack=first_only)
        first_only.close()
        w1_even = sb("w1_even", [P, KT, F])
        w3_even = sb("w3_even", [P, KT, F])
        w2_even = sb("w2_even", [P, FT, H])
        bias = sb("bias", [P, G, PROJ], stack=both)
        w_qkv = sb("w_qkv", [P, KT, WROWS], stack=both)
        w_o = sb("w_o", [P, QTILES, H], stack=both)
        kT = sb("kT", [P, S], stack=both)
        vT = sb("vT", [P, S], stack=both)
        v = sb("v", [P, QT, P], stack=both)
        probs = sb("probs", [P, N_PROB, S], stack=both)
        probsT = sb("probsT", [P, 2, 2, QT, S], stack=both)
        oT = sb("oT", [P, QTILES, S], stack=both)
        negmax = sb("negmax", [P, N_PROB], stack=both)
        rowsum = sb("rowsum", [P, N_PROB], stack=both)
        rinv = sb("rinv", [P, N_PROB], stack=both)
        q_hl = sb("q_hl", [P, 2 * QTILES, S], F32R, stack=second_only)
        k_hi = sb("k_hi", [P, 2, S], F32R, stack=second_only)
        k_lo = sb("k_lo", [P, 2, S], F32R, stack=second_only)
        second_only.close()
        both.close()
        w1_odd = sb("w1_odd", [P, KT, F])
        w3_odd = sb("w3_odd", [P, KT, F])
        w2_odd = sb("w2_odd", [P, FT, H])
        gated = sb("gated", [P, N_GATED, S])
        rectified = sb("rectified", [P, 2, S])
        w1_sb, w3_sb, w2_sb = (w1_even, w1_odd), (w3_even, w3_odd), (w2_even, w2_odd)

        x_loaded = sem("x_loaded")
        tables_loaded = sem("tables_loaded")
        consts_ready = sem("consts_ready")
        small_ready = sem("small_ready")
        acc_cleared = sem("acc_cleared")
        dve_step = sem("dve_step")
        root_asked = sem("root_asked")
        root_ready = sem("root_ready")
        rows_ready = sem("rows_ready")
        rows_turned = sem("rows_turned")
        hT_ready = sem("hT_ready")
        logits_ready = sem("logits_ready")
        e_shifted = sem("e_shifted")
        e_exp_ready = sem("e_exp_ready")
        weights_loaded = [sem("weights_loaded_even"), sem("weights_loaded_odd")]
        up_ready = sem("up_ready")
        relu_ready = sem("relu_ready")
        gated_ready = sem("gated_ready")
        down_done = sem("down_done")
        expert_added = sem("expert_added")
        stored = sem("stored")
        out_ready = sem("out_ready")

        def attention_sems(tag):
            names = ["w_loaded", "wo_loaded", "proj_psum_ready", "proj_evacuated", "cos_ready", "sin_ready",
                     "q_ready", "k_ready", "q_high", "k_high", "v_psum_ready", "v_ready", "scores_ready",
                     "max_ready", "probs_ready", "rinv_ready", "norm_ready", "pt_psum_ready", "pt_ready",
                     "o_psum_ready", "oT_ready", "y_psum_ready", "y_added"]
            return {n: sem(f"{n}_{tag}") for n in names}

        class Phase:
            def __init__(self, number, head, w_dram, o_dram):
                self.number = number
                self.first = number == 0
                self.sems = attention_sems("ab"[number])
                self.units = QROWS // head * QT
                self.group = self.units // QTILES
                self.w_dram, self.o_dram = w_dram, o_dram

        phases = [Phase(0, D1, wa_in, oa_in), Phase(1, D2, wb_in, ob_in)]
        PROBS0, PTPSUM0, PT0, OPSUM0 = N_SCORE, N_PROB, N_TURN, 2
        GATED0, DOWN0 = 2, N_GATED
        Y0, ADDED0 = 1, 1

        def steps(eng, body):
            with eng.Fori(0, STEPS - 1) as s:
                body(s, False)
            body(STEPS - 1, True)

        def projection_slot(ph, u):
            if u >= ph.units:
                return 3 + u - ph.units
            return u // ph.group if u % ph.group == ph.group - 1 and u // ph.group < 3 else None

        def values_slot(ph, u):
            n = u - LAG
            return n // ph.group if n >= 0 and n % ph.group == ph.group - 1 else None

        block = ctx.enter_context(nc.Block())

        @block.sync
        def _(sp):
            x_v = x_in.rearrange("(i p) h -> p i h", p=P)
            sp.dma_start(x[:, :, :], x_v).then_inc(x_loaded, 16)
            sp.dma_start(ln_w[:, :, :], ln_in).then_inc(tables_loaded, 16)
            sp.dma_start(bias[:, :, :], ba_in).then_inc(tables_loaded, 16)
            sp.dma_start(cosT[:, :], cos_in).then_inc(tables_loaded, 16)
            sp.dma_start(sinT[:, :], sin_in).then_inc(tables_loaded, 16)
            sp.dma_start(gate_w[:, :, :], gate_in.rearrange("(k p) e -> p k e", p=P)).then_inc(tables_loaded, 16)

            def load_w(ph, s):
                sp.dma_start(w_qkv[:, :, :], ph.w_dram[bass.ds((s % G) * H, H), :]
                             .rearrange("(k p) n -> p k n", p=P)).then_inc(ph.sems["w_loaded"], 16)

            def load_wo(ph, s):
                sp.dma_start(w_o[:, :, :], ph.o_dram[bass.ds((s % G) * QROWS, QROWS), :]
                             .rearrange("(k p) n -> p k n", p=P)).then_inc(ph.sems["wo_loaded"], 16)

            def load_expert(e, par):
                sp.dma_start(w1_sb[par][:, :, :], w1_in[bass.ds(e * H, H), :]
                             .rearrange("(k p) n -> p k n", p=P)).then_inc(weights_loaded[par], 16)
                sp.dma_start(w3_sb[par][:, :, :], w3_in[bass.ds(e * H, H), :]
                             .rearrange("(k p) n -> p k n", p=P)).then_inc(weights_loaded[par], 16)
                sp.dma_start(w2_sb[par][:, :, :], w2_in[bass.ds(e * F, F), :]
                             .rearrange("(k p) n -> p k n", p=P)).then_inc(weights_loaded[par], 16)

            for ph in phases:
                c = ph.sems
                load_w(ph, 0)
                load_wo(ph, 0)
                if not ph.first:
                    load_expert(0, 0)
                sp.wait_ge(c["proj_psum_ready"], PROJ)
                load_w(ph, 1)
                with sp.Fori(0, STEPS - 2) as s:
                    sp.wait_ge(c["proj_psum_ready"], PROJ * (s + 2))
                    load_w(ph, s + 2)
                    sp.wait_ge(c["y_psum_ready"], 2 * (s + 1))
                    load_wo(ph, s + 1)
                sp.wait_ge(c["y_psum_ready"], 2 * (STEPS - 1))
                load_wo(ph, STEPS - 1)
                sp.wait_ge(c["y_added"], Y0 + 2 * STEPS)
            load_expert(1, 1)
            with sp.Fori(0, E // 2 - 1) as pair:
                for par in range(2):
                    sp.wait_ge(down_done, DOWN0 + FT * TB * (2 * pair + par + 1))
                    load_expert(2 * pair + par + 2, par)
            sp.wait_ge(out_ready, 1)
            sp.dma_start(out.rearrange("(i p) h -> p i h", p=P), x[:, :, :]).then_inc(stored, 16)
            sp.wait_ge(stored, 16)

        @block.gpsimd
        def _(pool):
            pool.memset(identity[:, :], 0.0).then_inc(acc_cleared, 1)
            pool.memset(causal[:, :], 0.0).then_inc(acc_cleared, 1)
            pool.wait_ge(acc_cleared, 2)
            pool.affine_select(out=identity[:, :], in_=identity[:, :], compare_op=ALU.not_equal, fill=1.0,
                               base=0, pattern=[[-1, P]], channel_multiplier=1).then_inc(consts_ready, 1)
            pool.affine_select(out=causal[:, :], in_=causal[:, :], compare_op=ALU.is_ge, fill=MASKED,
                               base=0, pattern=[[-1, P]], channel_multiplier=1).then_inc(consts_ready, 1)
            pool.iota(iota_i[:, :, :], pattern=[[0, TILES], [1, E]], base=0, channel_multiplier=0)\
                .then_inc(consts_ready, 1)
            pool.memset(acc[:, :, :], 0.0).then_inc(acc_cleared, 1)
            pool.wait_ge(consts_ready, 3)
            pool.tensor_copy(identity_b[:, :], identity[:, :]).then_inc(small_ready, 1)
            pool.tensor_copy(causal_b[:, :], causal[:, :]).then_inc(small_ready, 1)
            pool.tensor_copy(iota_e[:, :, :], iota_i[:, :, :]).then_inc(small_ready, 1)

            c = phases[0].sems
            pool.wait_ge(tables_loaded, 5 * 16)

            def times_cosine(sp_, t):
                pool.wait_ge(c["proj_evacuated"], PROJ * sp_ + t + 1)
                pool.tensor_tensor(times_cos[:, t % 2, :], unroped[:, t % 2, :], cosT[:, :], ALU.mult)\
                    .then_inc(c["cos_ready"], 1)

            for t in range(T_K + 1):
                times_cosine(0, t)
            with pool.Fori(1, STEPS) as s:
                for t in range(T_K + 1):
                    times_cosine(s, t)

        @block.tensor
        def _(pe):
            def turn_rows(norm):
                for b in range(B):
                    pe.wait_ge(rows_ready, B * norm + b + 1)
                    for k in range(KT):
                        for i in range(QT):
                            mm = pe.transpose(bank[KT * b + k][:, i * P:(i + 1) * P],
                                              htok[:, QT * b + i, k * P:(k + 1) * P], identity[:, :])
                        mm.then_inc(rows_turned, 1)
                pe.wait_ge(hT_ready, B * KT * (norm + 1))

            def attention(ph):
                c = ph.sems

                def project(sp_, t):
                    if t == 0:
                        pe.wait_ge(c["w_loaded"], 16 * (sp_ + 1))
                    else:
                        pe.wait_ge(c["proj_evacuated"], PROJ * sp_ + t)
                    b = sp_ // G
                    for k in range(KT):
                        mm = pe.matmul(x_bank[:, :], w_qkv[:, k, t * P:(t + 1) * P],
                                       hT[:, k, bass.ds(b * S, S)], start=(k == 0), stop=(k == KT - 1))
                    mm.then_inc(c["proj_psum_ready"], 1)

                def turn_v(sp_):
                    pe.wait_ge(c["proj_evacuated"], PROJ * (sp_ + 1))
                    for i in range(QT):
                        mm = pe.transpose(o_bank[:, i * P:(i + 1) * P], vT[:, i * P:(i + 1) * P], identity[:, :])
                    mm.then_inc(c["v_psum_ready"], 1)

                def scores(s, u):
                    h, q = u // QT, u % QT
                    w = (q + 1) * P
                    dst = score_bank[u % N_SCORE]
                    if u % ph.group == 0:
                        pe.wait_ge(c["q_ready"], QTILES * s + u // ph.group + 1)
                    if u == 0:
                        pe.wait_ge(c["k_ready"], s + 1)
                    pe.wait_ge(c["probs_ready"], s * ph.units + u + 1)
                    if ph.first:
                        pe.matmul(dst[:, 0:w], qT[:, h, q * P:w], kT[:, 0:w], start=True, stop=False)
                    else:
                        kv = h // 4
                        pe.matmul(dst[:, 0:w], q_hl[:, h, q * P:w], k_hi[:, kv, 0:w], start=True, stop=False)
                        pe.matmul(dst[:, 0:w], q_hl[:, h, q * P:w], k_lo[:, kv, 0:w], start=False, stop=False)
                    pe.matmul(dst[:, q * P:w], identity_b[:, :], causal_b[:, :], start=False, stop=True)\
                        .then_inc(c["scores_ready"], 1)

                def turn(s, u):
                    q = u % QT
                    pe.wait_ge(c["norm_ready"], s * ph.units + u + 1)
                    pe.wait_ge(c["pt_ready"], s * ph.units + u + 1)
                    for k in range(q + 1):
                        mm = pe.transpose(turn_bank[u % N_TURN][:, k * P:(k + 1) * P],
                                          probs[:, u % N_PROB, k * P:(k + 1) * P], identity[:, :])
                    mm.then_inc(c["pt_psum_ready"], 1)

                def values(s, j):
                    if j == 0:
                        pe.wait_ge(c["v_ready"], s + 1)
                        pe.wait_ge(c["y_added"], Y0 + 2 * s)
                    else:
                        pe.wait_ge(c["oT_ready"], QTILES * s + j)
                    pe.wait_ge(c["pt_ready"], PT0 + s * ph.units + (j + 1) * ph.group)
                    for k in range(QT):
                        if ph.first:
                            mm = pe.matmul(o_bank[:, k * P:S], v[:, k, :], probsT[:, j % 2, 0, k, k * P:S],
                                           start=(k == 0), stop=(k == QT - 1))
                        else:
                            kv = j // 2
                            for i in range(2):
                                mm = pe.matmul(o_bank[i * D2:(i + 1) * D2, k * P:S],
                                               v[:, k, kv * D2:(kv + 1) * D2], probsT[:, j % 2, i, k, k * P:S],
                                               start=(k == 0), stop=(k == QT - 1))
                    mm.then_inc(c["o_psum_ready"], 1)

                def output(s, i, dst):
                    for q in range(2 * i, 2 * i + 2):
                        for j in range(QTILES):
                            mm = pe.matmul(dst[:, (q % 2) * H:(q % 2 + 1) * H], oT[:, j, q * P:(q + 1) * P],
                                           w_o[:, j, :], start=(j == 0), stop=(j == QTILES - 1))
                    mm.then_inc(c["y_psum_ready"], 1)

                pe.sem_inc(c["pt_psum_ready"], PTPSUM0)
                pe.sem_inc(c["o_psum_ready"], OPSUM0)
                for t in range(PROJ):
                    project(0, t)
                turn_v(0)

                def body(s, last):
                    for u in range(ph.units + LAG):
                        if u < ph.units:
                            scores(s, u)
                        if u >= LAG:
                            turn(s, u - LAG)
                        t = projection_slot(ph, u)
                        if t is not None and not last:
                            if t == 0:
                                pe.wait_ge(c["y_added"], Y0 + 2 * s)
                            project(s + 1, t)
                        j = values_slot(ph, u)
                        if j is not None:
                            values(s, j)
                    pe.wait_ge(c["wo_loaded"], 16 * (s + 1))
                    pe.wait_ge(c["oT_ready"], QTILES * (s + 1))
                    if last:
                        pe.wait_ge(c["y_added"], Y0 + 2 * s)
                    else:
                        pe.wait_ge(c["proj_evacuated"], PROJ * (s + 2))
                    output(s, 0, x_bank)
                    if not last:
                        turn_v(s + 1)
                        pe.wait_ge(c["v_ready"], s + 2)
                    output(s, 1, o_bank)
                steps(pe, body)

            pe.wait_ge(consts_ready, 2)
            pe.wait_ge(small_ready, 2)
            for ph in phases:
                turn_rows(ph.number)
                attention(ph)

            turn_rows(2)
            for i in range(TILES):
                for k in range(KT):
                    mm = pe.matmul(logit_bank[:, i * E:(i + 1) * E], hT[:, k, i * P:(i + 1) * P], gate_w[:, k, :],
                                   start=(k == 0), stop=(k == KT - 1))
            mm.then_inc(logits_ready, 1)

            pe.sem_inc(down_done, DOWN0)

            def expert_step(m, tb, par):
                def up(f):
                    pe.wait_ge(gated_ready, FT * m + f + 1)
                    for dst, w in ((up_bank[f % 2], w1_sb[par]), (lin_bank[f % 2], w3_sb[par])):
                        for k in range(KT):
                            mm = pe.matmul(dst[:, :], w[:, k, f * P:(f + 1) * P], hT[:, k, bass.ds(tb * 512, 512)],
                                           start=(k == 0), stop=(k == KT - 1))
                    mm.then_inc(up_ready, 1)

                def down(f):
                    if f == 0:
                        pe.wait_ge(expert_added, ADDED0 + m)
                    pe.wait_ge(gated_ready, GATED0 + FT * m + f + 1)
                    for q in range(QT):
                        mm = pe.matmul(down_bank[q // 2][:, (q % 2) * H:(q % 2 + 1) * H],
                                       gated[:, f % N_GATED, q * P:(q + 1) * P], w2_sb[par][:, f, :],
                                       start=(f == 0 and q % 2 == 0), stop=(f == FT - 1),
                                       skip_group_check=True)
                    mm.then_inc(down_done, 1)

                for f in range(FT):
                    up(f)
                    if f >= 1:
                        down(f - 1)
                down(FT - 1)

            with pe.Fori(0, E // 2) as pair:
                for par in range(2):
                    with pe.Fori(0, TB) as tb:
                        pe.wait_ge(weights_loaded[par], 48 * (pair + 1))
                        expert_step((2 * pair + par) * TB + tb, tb, par)

        @block.scalar
        def _(act):
            roots = [0]

            def root_of_square():
                roots[0] += 1
                act.wait_ge(root_asked, roots[0])
                act.activation(root[:, :], square[:, :], ACT.Sqrt).then_inc(root_ready, 1)

            def take_rows(norm):
                if norm == 0:
                    act.wait_ge(tables_loaded, 5 * 16)
                for b in range(B):
                    for k in range(KT):
                        act.wait_ge(rows_turned, B * KT * norm + KT * b + k + 1)
                        act.activation(hT[:, k, b * S:(b + 1) * S], bank[KT * b + k][:, :], ACT.Copy,
                                       scale=ln_w[:, norm, k:k + 1]).then_inc(hT_ready, 1)

            def attention(ph):
                c = ph.sems
                act.sem_inc(c["probs_ready"], PROBS0)
                act.sem_inc(c["pt_ready"], PT0)

                def take_projection(sp_, t, is_first):
                    act.wait_ge(c["proj_psum_ready"], PROJ * sp_ + t + 1)
                    if t == T_V:
                        if not is_first:
                            act.wait_ge(c["v_psum_ready"], sp_)
                        if ph.first:
                            act.activation(vT[:, :], x_bank[:, :], ACT.Identity,
                                           bias=bias[:, bass.ds(sp_ % G, 1), t])\
                                .then_inc(c["proj_evacuated"], 1)
                        else:
                            act.activation(vT[:, :], x_bank[:, :], ACT.Copy).then_inc(c["proj_evacuated"], 1)
                        return
                    if ph.first:
                        if t >= 2:
                            act.wait_ge(c["q_ready"], QTILES * sp_ + t - 1)
                        elif not is_first:
                            act.wait_ge(c["k_ready" if t == 0 else "q_ready"], (1 if t == 0 else QTILES) * sp_)
                        act.activation(unroped[:, t % 2, :], x_bank[:, :], ACT.Identity,
                                       bias=bias[:, bass.ds(sp_ % G, 1), t]).then_inc(c["proj_evacuated"], 1)
                        return
                    if t < T_K:
                        if not is_first:
                            act.wait_ge(c["scores_ready"], (sp_ - 1) * ph.units + (t + 1) * ph.group)
                        act.activation(q_hl[0:D2, 2 * t, :], x_bank[0:D2, :], ACT.Copy, scale=D2 ** -0.5)
                        act.activation(q_hl[D2:P, 2 * t + 1, :], x_bank[D2:P, :], ACT.Copy, scale=D2 ** -0.5)\
                            .then_inc(c["q_high"], 1)
                    else:
                        if not is_first:
                            act.wait_ge(c["scores_ready"], sp_ * ph.units)
                        for kv in range(2):
                            for half in range(2):
                                ins = act.activation(k_hi[half * D2:(half + 1) * D2, kv, :],
                                                     x_bank[kv * D2:(kv + 1) * D2, :], ACT.Copy)
                        ins.then_inc(c["k_high"], 1)

                def take_v(sp_):
                    act.wait_ge(c["v_psum_ready"], sp_ + 1)
                    act.activation(v[:, :, :], o_bank[:, :].rearrange("p (i d) -> p i d", i=QT), ACT.Copy)\
                        .then_inc(c["v_ready"], 1)

                def exponentials(s, u):
                    w = (u % QT + 1) * P
                    i = u % N_PROB
                    act.wait_ge(c["max_ready"], s * ph.units + u + 1)
                    act.wait_ge(c["pt_psum_ready"], s * ph.units + u + 1)
                    act.activation(probs[:, i, 0:w], score_bank[u % N_SCORE][:, 0:w], ACT.Exp,
                                   bias=negmax[:, i:i + 1], accum_out=rowsum[:, i:i + 1])\
                        .then_inc(c["probs_ready"], 1)

                def take_turned(s, u):
                    q = u % QT
                    j = u // ph.group
                    i = 0 if ph.first else u // QT % 2
                    act.wait_ge(c["pt_psum_ready"], PTPSUM0 + s * ph.units + u + 1)
                    if u % ph.group == 0:
                        act.wait_ge(c["o_psum_ready"], QTILES * s + j + 1)
                    act.activation(probsT[:, j % 2, i, 0:q + 1, q * P:(q + 1) * P],
                                   turn_bank[u % N_TURN][:, 0:(q + 1) * P].rearrange("p (k n) -> p k n", n=P),
                                   ACT.Copy).then_inc(c["pt_ready"], 1)

                for t in range(PROJ):
                    take_projection(0, t, True)
                take_v(0)

                def body(s, last):
                    for u in range(ph.units + LAG):
                        if u < ph.units:
                            exponentials(s, u)
                        if u >= LAG:
                            take_turned(s, u - LAG)
                        t = projection_slot(ph, u)
                        if t is not None and not last:
                            take_projection(s + 1, t, False)
                    if not last:
                        take_v(s + 1)
                steps(act, body)

            root_of_square()
            root_of_square()
            take_rows(0)
            attention(phases[0])
            for _ in range(3):
                root_of_square()
            take_rows(1)
            attention(phases[1])
            root_of_square()
            take_rows(2)
            act.wait_ge(e_shifted, 1)
            act.activation(e_prob[:, :, :], pick[:, :, :], ACT.Exp).then_inc(e_exp_ready, 1)

            def expert_step(m):
                for f in range(FT):
                    act.wait_ge(up_ready, FT * m + f + 1)
                    act.activation(rectified[:, f % 2, :], up_bank[f % 2][:, :], ACT.Relu).then_inc(relu_ready, 1)

            with act.Fori(0, E * TB) as m:
                expert_step(m)
            root_of_square()

        @block.vector
        def _(dve):
            count = [0, 0]

            def link(ins):
                count[0] += 1
                ins.then_inc(dve_step, 1)
                dve.wait_ge(dve_step, count[0])

            def moments(src):
                for i in range(TILES):
                    ins = dve.bn_stats(stats[:, i, :], src[:, i, :])
                link(ins)
                for i in range(TILES):
                    ins = dve.bn_aggr(mv[:, i, :], stats[:, i, :])
                link(ins)
            mean, var = mv[:, :, 0], mv[:, :, 1]

            def inverse_root(dst, src, eps):
                count[1] += 1
                dve.tensor_scalar(square[:, :], src, eps, None, ALU.add).then_inc(root_asked, 1)
                dve.wait_ge(root_ready, count[1])
                link(dve.reciprocal(dst[:, :], root[:, :]))

            def minus_mean_times(inv):
                link(dve.scalar_tensor_tensor(out=shift[:, :], in0=mean, scalar=-1.0, in1=inv[:, :],
                                              op0=ALU.mult, op1=ALU.mult))

            def scaled(dst, src, factor, sum_sem=None):
                for i in range(TILES):
                    ins = dve.tensor_scalar(dst[:, i, :], src[:, i, :], factor[:, i:i + 1], shift[:, i:i + 1],
                                            ALU.mult, ALU.add)
                    if sum_sem is not None and i % QT == QT - 1:
                        ins.then_inc(sum_sem, 1)
                if sum_sem is None:
                    link(ins)

            def times(dst, src, factor):
                for i in range(TILES):
                    ins = dve.tensor_scalar(dst[:, i, :], src[:, i, :], factor[:, i:i + 1], None, ALU.mult)
                    if i % QT == QT - 1:
                        ins.then_inc(rows_ready, 1)

            def norm_of_norm(eps):
                moments(x)
                inverse_root(inv1, var, LN_EPS)
                link(dve.tensor_tensor(scale[:, :], inv1[:, :], inv1[:, :], ALU.mult))
                link(dve.tensor_tensor(scale[:, :], scale[:, :], var, ALU.mult))
                inverse_root(inv2, scale[:, :], eps)

            def add_norm_of_acc():
                moments(acc)
                inverse_root(inv1, var, LN_EPS)
                minus_mean_times(inv1)
                scaled(acc, acc, inv1)
                return dve.tensor_tensor(x[:, :, :], x[:, :, :], acc[:, :, :], ALU.add)

            def attention(ph):
                c = ph.sems

                def take_projection(sp_, t, is_first):
                    if t == T_V:
                        return
                    queries = t < T_K

                    def wait_unused():
                        if not is_first:
                            dve.wait_ge(c["scores_ready"], (sp_ - 1) * ph.units + (t + 1) * ph.group if queries
                                        else sp_ * ph.units)
                    if ph.first:
                        i = t % 2
                        dve.wait_ge(c["proj_evacuated"], PROJ * sp_ + t + 1)
                        dve.tensor_tensor(times_sin[0:D1 // 2, i, :], unroped[D1 // 2:D1, i, :],
                                          sinT[D1 // 2:D1, :], ALU.mult)
                        dve.tensor_tensor(times_sin[D1 // 2:D1, i, :], unroped[0:D1 // 2, i, :],
                                          sinT[0:D1 // 2, :], ALU.mult).then_inc(c["sin_ready"], 1)
                        dve.wait_ge(c["sin_ready"], (T_K + 1) * sp_ + t + 1)
                        dve.wait_ge(c["cos_ready"], (T_K + 1) * sp_ + t + 1)
                        wait_unused()
                        dst = qT[:, t, :] if queries else kT[:, :]
                        dve.tensor_tensor(dst, times_cos[:, i, :], times_sin[:, i, :], ALU.add)\
                            .then_inc(c["q_ready" if queries else "k_ready"], 1)
                        return
                    if queries:
                        dve.wait_ge(c["q_high"], QTILES * sp_ + t + 1)
                        dve.scalar_tensor_tensor(out=q_hl[D2:P, 2 * t, :], in0=x_bank[0:D2, :], scalar=D2 ** -0.5,
                                                 in1=q_hl[0:D2, 2 * t, :].bitcast(F32),
                                                 op0=ALU.mult, op1=ALU.subtract)
                        dve.scalar_tensor_tensor(out=q_hl[0:D2, 2 * t + 1, :], in0=x_bank[D2:P, :],
                                                 scalar=D2 ** -0.5, in1=q_hl[D2:P, 2 * t + 1, :].bitcast(F32),
                                                 op0=ALU.mult, op1=ALU.subtract).then_inc(c["q_ready"], 1)
                    else:
                        dve.wait_ge(c["k_high"], sp_ + 1)
                        for kv in range(2):
                            part = slice(kv * D2, (kv + 1) * D2)
                            for half in range(2):
                                ins = dve.tensor_tensor(k_lo[half * D2:(half + 1) * D2, kv, :], x_bank[part, :],
                                                        k_hi[part, kv, :].bitcast(F32), ALU.subtract)
                        ins.then_inc(c["k_ready"], 1)
                    dve.wait_ge(c["q_ready" if queries else "k_ready"], QTILES * sp_ + t + 1 if queries else sp_ + 1)
                    dve.sem_inc(c["proj_evacuated"], 1)

                def maximum(s, u):
                    i = u % N_PROB
                    dve.wait_ge(c["scores_ready"], s * ph.units + u + 1)
                    dve.tensor_reduce(negmax[:, i:i + 1], score_bank[u % N_SCORE][:, 0:(u % QT + 1) * P], AX_X,
                                      ALU.max, negate=True).then_inc(c["max_ready"], 1)

                def normalise(s, u):
                    i = u % N_PROB
                    w = (u % QT + 1) * P
                    dve.wait_ge(c["probs_ready"], PROBS0 + s * ph.units + u + 1)
                    dve.reciprocal(rinv[:, i:i + 1], rowsum[:, i:i + 1]).then_inc(c["rinv_ready"], 1)
                    dve.wait_ge(c["rinv_ready"], s * ph.units + u + 1)
                    dve.tensor_scalar(probs[:, i, 0:w], probs[:, i, 0:w], rinv[:, i:i + 1], None, ALU.mult)\
                        .then_inc(c["norm_ready"], 1)

                def take_values(s, j):
                    dve.wait_ge(c["o_psum_ready"], OPSUM0 + QTILES * s + j + 1)
                    dve.tensor_copy(oT[:, j, :], o_bank[:, :]).then_inc(c["oT_ready"], 1)

                def add_output(s, i, src):
                    dve.wait_ge(c["y_psum_ready"], 2 * s + i + 1)
                    dve.wait_ge(c["y_added"], Y0 + 2 * s)
                    b = s // G
                    dst = acc[:, bass.ds(b * QT + 2 * i, 2), :]
                    dve.tensor_tensor(dst, dst, src[:, :].rearrange("p (i h) -> p i h", i=2), ALU.add)\
                        .then_inc(c["y_added"], 1)

                dve.sem_inc(c["y_added"], Y0)
                for t in range(PROJ):
                    take_projection(0, t, True)

                def body(s, last):
                    for u in range(ph.units + LAG):
                        if u < ph.units:
                            maximum(s, u)
                        if 1 <= u <= ph.units:
                            normalise(s, u - 1)
                        t = projection_slot(ph, u)
                        if t is not None and not last:
                            take_projection(s + 1, t, False)
                        j = values_slot(ph, u)
                        if j is not None:
                            take_values(s, j)
                    add_output(s, 0, x_bank)
                    add_output(s, 1, o_bank)
                steps(dve, body)
                dve.wait_ge(c["y_added"], Y0 + 2 * STEPS)

            dve.wait_ge(x_loaded, 16)
            norm_of_norm(RMS_A_EPS)
            link(dve.tensor_tensor(scale[:, :], inv1[:, :], inv2[:, :], ALU.mult))
            minus_mean_times(scale)
            scaled(htok, x, scale, rows_ready)
            dve.wait_ge(acc_cleared, 3)
            attention(phases[0])

            link(add_norm_of_acc())
            norm_of_norm(RMS_B_EPS)
            minus_mean_times(inv1)
            scaled(acc, x, inv1)
            times(htok, acc, inv2)
            attention(phases[1])

            moments(acc)
            link(dve.tensor_tensor(scale[:, :], mean, mean, ALU.mult))
            link(dve.tensor_tensor(scale[:, :], scale[:, :], var, ALU.add))
            inverse_root(inv1, scale[:, :], RMS_B_EPS)
            times(htok, acc, inv1)

            dve.sem_inc(gated_ready, GATED0)
            dve.sem_inc(expert_added, ADDED0)
            dve.wait_ge(logits_ready, 1)
            logits = logit_bank[:, 0:TILES * E].rearrange("p (i e) -> p i e", e=E)
            link(dve.tensor_copy(pick[:, :, :], logits))
            link(dve.tensor_reduce(e_max[:, :], pick[:, :, :], AX_X, ALU.max))
            link(dve.tensor_tensor(pick[:, :, :], pick[:, :, :],
                                   e_max[:, :].unsqueeze(2).broadcast_to([P, TILES, E]), ALU.subtract))
            dve.sem_inc(e_shifted, 1)
            dve.wait_ge(e_exp_ready, 1)
            link(dve.tensor_reduce(e_sum[:, :], e_prob[:, :, :], AX_X, ALU.add))
            link(dve.reciprocal(e_sum[:, :], e_sum[:, :]))
            link(dve.tensor_tensor(e_prob[:, :, :], e_prob[:, :, :],
                                   e_sum[:, :].unsqueeze(2).broadcast_to([P, TILES, E]), ALU.mult))
            for i in range(TILES):
                ins = dve.max(e_top[:, i, :], e_prob[:, i, :])
            link(ins)
            for i in range(TILES):
                ins = dve.max_index(e_topi[:, i, :], e_top[:, i, :], e_prob[:, i, :])
            link(ins)
            link(dve.tensor_copy(e_topf[:, :, :], e_topi[:, :, :]))
            link(dve.tensor_tensor(e_sum[:, :], e_top[:, :, 0], e_top[:, :, 1], ALU.add))
            link(dve.reciprocal(e_sum[:, :], e_sum[:, :]))
            dve.wait_ge(small_ready, 3)
            for n in range(2):
                link(dve.tensor_tensor(e_max[:, :], e_top[:, :, n], e_sum[:, :], ALU.mult))
                dst = combine if n == 0 else pick
                link(dve.tensor_tensor(dst[:, :, :], iota_e[:, :, :],
                                       e_topf[:, :, n:n + 1].broadcast_to([P, TILES, E]), ALU.is_equal))
                link(dve.tensor_tensor(dst[:, :, :], dst[:, :, :],
                                       e_max[:, :].unsqueeze(2).broadcast_to([P, TILES, E]), ALU.mult))
            link(dve.tensor_tensor(combine[:, :, :], combine[:, :, :], pick[:, :, :], ALU.add))

            flat = combine[:, :, :].rearrange("p i e -> p (i e)")

            def expert_step(m, e, tb):
                for f in range(FT):
                    dve.wait_ge(relu_ready, FT * m + f + 1)
                    dve.wait_ge(down_done, FT * m + f + 1)
                    dve.tensor_tensor(gated[:, f % N_GATED, :], lin_bank[f % 2][:, :], rectified[:, f % 2, :],
                                      ALU.mult).then_inc(gated_ready, 1)
                dve.wait_ge(down_done, DOWN0 + FT * (m + 1))
                dve.wait_ge(expert_added, ADDED0 + m)
                for q in range(QT):
                    dst = acc[:, bass.ds(tb * QT + q, 1), :].rearrange("p i h -> p (i h)")
                    ins = dve.scalar_tensor_tensor(out=dst, in0=down_bank[q // 2][:, (q % 2) * H:(q % 2 + 1) * H],
                                                   scalar=flat[:, bass.ds((tb * QT + q) * E + e, 1)], in1=dst,
                                                   op0=ALU.mult, op1=ALU.add)
                ins.then_inc(expert_added, 1)

            with dve.Fori(0, E // 2) as pair:
                for par in range(2):
                    with dve.Fori(0, TB) as tb:
                        expert_step((2 * pair + par) * TB + tb, 2 * pair + par, tb)
            dve.wait_ge(expert_added, ADDED0 + E * TB)
            add_norm_of_acc().then_inc(out_ready, 1)

        del block


def kernel(**inputs):
    import numpy as np
    import concourse.bacc as bacc
    from concourse.bass_utils import run_bass_kernel_spmd

    a = {k: np.asarray(v) for k, v in inputs.items()}

    def tiles(n, count):
        return a[n].reshape(G, count, H).transpose(0, 2, 1)

    def columns(n, count):
        return a[n].reshape(H, G, count).transpose(1, 0, 2)

    inv_freq = (np.float32(1.0) / np.float32(10000.0) ** (np.arange(0, D1, 2, dtype=np.float32) / np.float32(D1)))
    angle = (np.arange(S, dtype=np.float32)[:, None] * inv_freq.astype(np.float32)).T
    half_scale = float(D1) ** -0.25
    cos, sin = np.cos(angle.astype(np.float64)) * half_scale, np.sin(angle.astype(np.float64)) * half_scale
    arrays = {
        "x_in": a["L0_attn_x"].reshape(T, H),
        "cos_in": np.concatenate([cos, cos]).astype(np.float32),
        "sin_in": np.concatenate([sin, -sin]).astype(np.float32),
        "wa_in": np.concatenate([tiles("L0_attn_q_project", QROWS), tiles("L0_attn_k_project", P),
                                 tiles("L0_attn_v_project", P)], axis=2).reshape(G * H, WROWS),
        "ba_in": np.concatenate([a["L0_attn_q_bias"].reshape(G, QTILES, P), a["L0_attn_k_bias"].reshape(G, 1, P),
                                 a["L0_attn_v_bias"].reshape(G, 1, P)], axis=1).transpose(2, 0, 1),
        "oa_in": a["L0_attn_o_project"].T,
        "wb_in": np.concatenate([columns("L0_ffn_wq", QROWS), columns("L0_ffn_wk", P),
                                 columns("L0_ffn_wv", P)], axis=2).reshape(G * H, WROWS),
        "ob_in": a["L0_ffn_wo"],
        "ln_in": np.stack([a["L0_attn_ln_weight"], a["L0_ffn_ln1_w"], a["L0_ffn_ln2_w"]])
        .reshape(3, KT, P).transpose(2, 0, 1),
        "gate_in": a["L0_ffn_gate_w"],
        "w1_in": a["L0_ffn_w1"].reshape(E * H, F),
        "w2_in": a["L0_ffn_w2"].reshape(E * F, H),
        "w3_in": a["L0_ffn_w3"].reshape(E * H, F),
    }
    arrays = {k: np.ascontiguousarray(v) for k, v in arrays.items()}
    nc = bacc.Bacc("TRN2", target_bir_lowering=False, num_devices=1)
    args = {k: nc.dram_tensor(f"{k}_dram", v.shape, mybir.dt.from_np(v.dtype), kind="ExternalInput").ap()
            for k, v in arrays.items()}
    result = nc.dram_tensor("result_dram", (T, H), F32, kind="ExternalOutput").ap()
    program(nc, out=result, **args)
    r = run_bass_kernel_spmd(nc, [{f"{k}_dram": v for k, v in arrays.items()}], core_ids=[0])
    return r.results[0]["result_dram"].reshape(B, S, H)
```

```python
from contextlib import ExitStack

import concourse.bass as bass
from concourse import mybir

F32 = mybir.dt.float32
F32R = mybir.dt.float32r
BF16 = mybir.dt.bfloat16
I32 = mybir.dt.int32
U32 = mybir.dt.uint32
ALU = mybir.AluOpType
ACT = mybir.ActivationFunctionType
AX_X = mybir.AxisListType.X

P = 128
B, S, H = 4, 512, 256
T = B * S
TILES = T // P
KT = H // P
QT = S // P
G = 4
QROWS = 512
QTILES = QROWS // P
WROWS = QROWS + 2 * P
PROJ = WROWS // P
T_K, T_V = QTILES, QTILES + 1
STEPS = B * G
D1, D2 = 128, 64
E, F = 8, 1024
FT = F // P
TOPK = 2
SLOTS = 256
BLOCKS = (TOPK * T + E * (SLOTS - 1)) // SLOTS
SA = SLOTS // P
LN_EPS = 1e-5
RMS_A_EPS = 1e-6
RMS_B_EPS = 1e-5
MASKED = -1e30
Q_ORDER = (0, 1, 3, 2)
LAG = 6
VALUES_LAG = 2
N_SCORE = 4
N_PROB = 8
N_TURN = 2
DOWN_LAG = 3
N_UP = 4
SPLIT_LAG = 4
N_GATED = 4


def program(nc, x_in, cos_in, sin_in, wa_in, ba_in, oa_in,
            wb_in, ob_in, ln_in, gate_in, w1_in, w2_in, w3_in, out):
    with ExitStack() as ctx:
        def sb(name, shape, dt=F32, stack=ctx):
            return stack.enter_context(nc.sbuf_tensor(name, shape, dt))

        def sem(name):
            return ctx.enter_context(nc.semaphore(name))

        bank = [ctx.enter_context(nc.psum_tensor(f"bank{i}", [P, 512], F32)) for i in range(8)]
        score_bank, turn_bank, o_bank, x_bank = bank[0:4], bank[4:6], bank[6], bank[7]
        up_bank, down_bank, router_bank, slot_bank = bank[0:4], bank[4:6], bank[6], bank[7]

        slot_rows = nc.dram_tensor("slot_rows", (BLOCKS * SLOTS, H), F32).ap()
        slot_results = nc.dram_tensor("slot_results", (BLOCKS * SLOTS, H), F32).ap()

        x = sb("x", [P, TILES, H])
        acc = sb("acc", [P, TILES, H])
        second_keys = ExitStack()
        k_hi = sb("k_hi", [P, 2, 2, S], F32R, stack=second_keys)
        k_lo = sb("k_lo", [P, 2, 2, S], F32R, stack=second_keys)
        second_keys.close()
        htok = sb("htok", [P, TILES, H])
        hT = sb("hT", [P, KT, T])
        identity = sb("identity", [P, P])
        causal = sb("causal", [P, P])
        identity_b = sb("identity_b", [P, P], BF16)
        causal_b = sb("causal_b", [P, P], BF16)
        iota_i = sb("iota_i", [P, TILES, E], I32)
        iota_e = sb("iota_e", [P, TILES, E])
        ln_w = sb("ln_w", [P, 3, KT])
        gate_w = sb("gate_w", [P, KT, E])
        ones = sb("ones", [P, 1])
        stats = sb("stats", [P, TILES, 6])
        mv = sb("mv", [P, TILES, 2])
        square = sb("square", [P, TILES])
        root = sb("root", [P, TILES])
        inv1 = sb("inv1", [P, TILES])
        inv2 = sb("inv2", [P, TILES])
        scale = sb("scale", [P, TILES])
        shift = sb("shift", [P, TILES])
        e_max = sb("e_max", [P, TILES])
        e_sum = sb("e_sum", [P, TILES])
        e_prob = sb("e_prob", [P, TILES, E])
        e_top = sb("e_top", [P, TILES, E])
        e_topi = sb("e_topi", [P, TILES, E], U32)
        e_topf = sb("e_topf", [P, TILES, E])
        pick = sb("pick", [P, TILES, E])
        choice = [sb(f"choice{n}", [P, TILES, E]) for n in range(TOPK)]
        share = [sb(f"share{n}", [P, TILES]) for n in range(TOPK)]
        chosen_b = sb("chosen_b", [P, TILES * E], BF16)
        earlier_b = sb("earlier_b", [P, P], BF16)
        ones_b = sb("ones_b", [P, P], BF16)
        run = sb("run", [P, TILES + 1, E])
        whole_i = sb("whole_i", [P, E], I32)
        whole = sb("whole", [P, E])
        first_slot = sb("first_slot", [P, E + 1])
        place = sb("place", [P, TILES, E])
        slot_f = sb("slot_f", [P, TILES])
        slot_of = [sb(f"slot_of{n}", [P, TILES], U32) for n in range(TOPK)]
        block_start_i = sb("block_start_i", [P, BLOCKS, E], I32)
        block_start = sb("block_start", [P, BLOCKS, E])
        passed = sb("passed", [P, BLOCKS, E])
        block_expert_f = sb("block_expert_f", [P, BLOCKS])
        block_expert = sb("block_expert", [P, BLOCKS], I32)

        both, first_only, second_only = ExitStack(), ExitStack(), ExitStack()
        bias = sb("bias", [P, G, PROJ], stack=both)
        w_qkv = sb("w_qkv", [P, 2, KT, WROWS], stack=both)
        w_o = sb("w_o", [P, QTILES, H], stack=both)
        projected = sb("projected", [P, 2, S], stack=both)
        vT = sb("vT", [P, S], stack=both)
        v = sb("v", [P, 2, QT, P], stack=both)
        probs = sb("probs", [P, N_PROB, S], stack=both)
        probsT = sb("probsT", [P, 2, 2, QT, S], stack=both)
        oT = sb("oT", [P, QTILES, S], stack=both)
        negmax = sb("negmax", [P, N_PROB], stack=both)
        rowsum = sb("rowsum", [P, N_PROB], stack=both)
        rinv = sb("rinv", [P, N_PROB], stack=both)
        cosT = sb("cosT", [P, S], stack=first_only)
        sinT = sb("sinT", [P, S], stack=first_only)
        times_cos = sb("times_cos", [P, 2, S], stack=first_only)
        times_sin = sb("times_sin", [P, 2, S], stack=first_only)
        qT = sb("qT", [P, QTILES, S], stack=first_only)
        kT = sb("kT", [P, 2, S], stack=first_only)
        first_only.close()
        q_hl = sb("q_hl", [P, 2 * QTILES, S], F32R, stack=second_only)
        second_only.close()
        both.close()
        w13 = [sb(f"w13_{name}", [P, 2, KT, F]) for name in ("even", "odd")]
        w2 = [sb(f"w2_{name}", [P, FT, H]) for name in ("even", "odd")]
        w13_hi = sb("w13_hi", [P, 2, KT, F], F32R)
        w13_lo = sb("w13_lo", [P, 2, KT, F], F32R)
        w2_hi = sb("w2_hi", [P, FT, H], F32R)
        w2_lo = sb("w2_lo", [P, FT, H], F32R)
        rectified = sb("rectified", [P, N_UP, SLOTS])
        gated = sb("gated", [P, N_GATED, SLOTS])
        gated_hi = sb("gated_hi", [P, N_GATED, SLOTS], F32R)
        gated_lo = sb("gated_lo", [P, N_GATED, SLOTS], F32R)
        slot_tok = sb("slot_tok", [P, 2, SA, H])
        slot_hi = sb("slot_hi", [P, 2, KT, SLOTS], F32R)
        slot_lo = sb("slot_lo", [P, 2, KT, SLOTS], F32R)
        result = sb("result", [P, 2, SA, H])

        hT_rows = hT[:, :, :].rearrange("p k (i h) -> p (k i) h", h=H)

        x_loaded = sem("x_loaded")
        tables_loaded = sem("tables_loaded")
        consts_ready = sem("consts_ready")
        small_ready = sem("small_ready")
        acc_cleared = sem("acc_cleared")
        dve_step = sem("dve_step")
        root_asked = sem("root_asked")
        root_ready = sem("root_ready")
        rows_ready = sem("rows_ready")
        rows_turned = sem("rows_turned")
        hT_ready = sem("hT_ready")
        rows_cleared = sem("rows_cleared")
        logits_ready = sem("logits_ready")
        e_shifted = sem("e_shifted")
        e_exp_ready = sem("e_exp_ready")
        chosen_ready = sem("chosen_ready")
        ranks_ready = sem("ranks_ready")
        experts_ready = sem("experts_ready")
        slots_ready = sem("slots_ready")
        scattered = sem("scattered")
        weights_loaded = [sem("weights_even_loaded"), sem("weights_odd_loaded")]
        block_loaded = [sem("block_even_loaded"), sem("block_odd_loaded")]
        block_turned = sem("block_turned")
        block_high_ready = sem("block_high_ready")
        block_T_ready = sem("block_T_ready")
        w13_high_ready = sem("w13_high_ready")
        w13_ready = sem("w13_ready")
        w2_high_ready = sem("w2_high_ready")
        w2_ready = sem("w2_ready")
        product_ready = sem("product_ready")
        gated_high_ready = sem("gated_high_ready")
        up_ready = sem("up_ready")
        relu_ready = sem("relu_ready")
        gated_ready = sem("gated_ready")
        down_done = sem("down_done")
        result_ready = sem("result_ready")
        result_stored = [sem("result_even_stored"), sem("result_odd_stored")]
        gathered = [sem(f"gathered{b}") for b in range(B)]
        stored = sem("stored")
        out_ready = sem("out_ready")

        def attention_sems(tag):
            names = ["w_even_loaded", "w_odd_loaded", "wo_loaded", "proj_psum_ready", "x_bank_empty", "cos_ready", "sin_ready",
                     "high_ready", "q_ready", "k_ready", "v_psum_ready", "scores_ready", "max_ready", "probs_ready",
                     "rinv_ready", "norm_ready", "pt_psum_ready", "pt_ready", "o_psum_ready", "o_bank_empty",
                     "y_psum_ready"]
            return {n: sem(f"{n}_{tag}") for n in names}

        class Phase:
            def __init__(self, number, head, w_dram, o_dram, slots):
                self.number = number
                self.first = number == 0
                self.sems = attention_sems("ab"[number])
                self.units = QROWS // head * QT
                self.group = self.units // QTILES
                self.w_dram, self.o_dram = w_dram, o_dram
                self.slots = {u: list(ev) for u, ev in slots.items()}
                for j in range(QTILES):
                    u = (j + 1) * self.group - 1 + LAG + VALUES_LAG
                    self.slots.setdefault(u % self.units, []).append(("values", j, -(u // self.units)))

            def events(self, u, kind):
                return [e for e in self.slots.get(u, []) if kinds[kind](e)]

            def before(self, of, event, kind):
                n = 0
                for u in range(self.units):
                    for e in self.slots.get(u, []):
                        if e == event:
                            return n
                        n += kinds[kind](e) and e[2] in of
                raise ValueError(event)

            def per_step(self, of, kind):
                return sum(kinds[kind](e) and e[2] in of for ev in self.slots.values() for e in ev)

            def number_of(self, s, event, kind):
                start = PROLOGUE[kind]
                if isinstance(s, int) and s == 0:
                    return start + self.before((0, 1), event, kind)
                if isinstance(s, int) and s == STEPS - 1:
                    of = (-1, 0)
                elif isinstance(s, int) and s == STEPS:
                    of = (-1,)
                else:
                    of = (-1, 0, 1)
                full = self.per_step((-1, 0, 1), kind)
                start += self.per_step((0, 1), kind)
                if isinstance(s, int) and s == STEPS:
                    return (start + full * (STEPS - 2) + self.per_step((-1, 0), kind)
                            + self.before(of, event, kind))
                return full * (s - 1) + start + self.before(of, event, kind)

            def parity_of(self, s, parity, event):
                return self.number_of(s if isinstance(s, int) else 2 - parity, event, "rotate") % 2

            def two_before(self, s, event):
                row = [e for u in sorted(self.slots) for e in self.events(u, "rotate")]
                n = row.index(event)
                _, t, d = row[n - 2]
                d -= n < 2
                return ("k_ready", s + d + 1) if t == T_K else ("q_ready", QTILES * (s + d) + t + 1)

        kinds = {
            "x": lambda e: e[0] in ("project", "output"),
            "o": lambda e: e[0] in ("values", "turn_v"),
            "project": lambda e: e[0] == "project",
            "rotate": lambda e: e[0] == "project" and e[1] != T_V,
        }
        FIRST_TILES = (T_K, 0, 1, 2, T_V)
        PROLOGUE = {"x": 5, "o": 1, "project": 5, "rotate": 4}

        phases = [
            Phase(0, D1, wa_in, oa_in, {
                0: [("project", 3, 0)], 2: [("project", T_K, 1)], 4: [("project", 0, 1)], 6: [("project", T_V, 1)],
                8: [("output", 0, -1)], 9: [("output", 1, -1)], 10: [("project", 1, 1)], 12: [("project", 2, 1)],
                13: [("turn_v", 0, 1)]}),
            Phase(1, D2, wb_in, ob_in, {
                0: [("project", 3, 0)], 2: [("project", T_K, 1)], 5: [("project", T_V, 1)],
                9: [("output", 0, -1)], 11: [("output", 1, -1)], 13: [("project", 0, 1)],
                18: [("project", 1, 1)], 26: [("project", 2, 1)], 28: [("turn_v", 0, 1)]}),
        ]
        PROBS0, PTPSUM0, PT0, OPSUM0 = N_SCORE, N_PROB, N_TURN, 2
        PRODUCT0, DOWN0, RESULT0 = N_UP, FT, 2

        def steps(eng, slot, ph):
            def step(s, parity, of, upto=ph.units):
                for u in range(upto):
                    slot(s, parity, u, of)
            step(0, 0, (0, 1))
            with eng.Fori(0, (STEPS - 2) // 2) as pair:
                step(2 * pair + 1, 1, (-1, 0, 1))
                step(2 * pair + 2, 0, (-1, 0, 1))
            step(STEPS - 1, 1, (-1, 0))
            step(STEPS, 0, (-1,), max(u for u, ev in ph.slots.items() if any(e[2] == -1 for e in ev)) + 1)

        def unit_at(ph, s, u, back, of):
            if u >= back:
                return (s, u - back) if 0 in of else None
            return (s - 1, ph.units + u - back) if -1 in of else None

        block = ctx.enter_context(nc.Block())

        @block.sync
        def _(sp):
            x_v = x_in.rearrange("(i p) h -> p i h", p=P)
            sp.dma_start(x[:, :, :], x_v).then_inc(x_loaded, 16)
            sp.dma_start(ln_w[:, :, :], ln_in).then_inc(tables_loaded, 16)
            sp.dma_start(bias[:, :, :], ba_in).then_inc(tables_loaded, 16)
            sp.dma_start(cosT[:, :], cos_in).then_inc(tables_loaded, 16)
            sp.dma_start(sinT[:, :], sin_in).then_inc(tables_loaded, 16)
            sp.dma_start(gate_w[:, :, :], gate_in.rearrange("(k p) e -> p k e", p=P)).then_inc(tables_loaded, 16)

            def load_w(ph, s, parity):
                sp.dma_start(w_qkv[:, parity, :, :],
                             ph.w_dram[bass.ds((s % G) * H, H), :].rearrange("(k p) n -> p k n", p=P))\
                    .then_inc(ph.sems["w_odd_loaded" if parity else "w_even_loaded"], 16)

            def load_wo(ph, s):
                sp.dma_start(w_o[:, :, :], ph.o_dram[bass.ds((s % G) * QROWS, QROWS), :]
                             .rearrange("(k p) n -> p k n", p=P)).then_inc(ph.sems["wo_loaded"], 16)

            def load_expert(j, par):
                e = sp.value_load(block_expert[0:1, bass.ds(j, 1)], min_val=0, max_val=E - 1)
                for dst, src, rows in ((w13[par][:, 0, :, :], w1_in, H), (w13[par][:, 1, :, :], w3_in, H),
                                       (w2[par][:, :, :], w2_in, F)):
                    sp.dma_start(dst, src[bass.ds(e * rows, rows), :].rearrange("(k p) n -> p k n", p=P))\
                        .then_inc(weights_loaded[par], 16)

            def load_block(j, par):
                sp.dma_start(slot_tok[:, par, :, :], slot_rows[bass.ds(j * SLOTS, SLOTS), :]
                             .rearrange("(a p) h -> p a h", p=P)).then_inc(block_loaded[par], 16)

            def store_result(j, par):
                sp.wait_ge(result_ready, RESULT0 + j + 1)
                sp.dma_start(slot_results[bass.ds(j * SLOTS, SLOTS), :].rearrange("(a p) h -> p a h", p=P),
                             result[:, par, :, :]).then_inc(result_stored[par], 16)

            rows = slot_rows.rearrange("(p r) h -> p (r h)", p=P)
            width = rows.shape[1]
            sp.wait_ge(acc_cleared, 3)
            pieces = list(range(0, width, TILES * H))
            for at in pieces:
                n = min(TILES * H, width - at)
                sp.dma_start(rows[:, at:at + n], acc[:, :, :].rearrange("p i h -> p (i h)")[:, 0:n])\
                    .then_inc(rows_cleared, 16)

            for ph in phases:
                c = ph.sems
                load_w(ph, 0, 0)
                load_wo(ph, 0)
                load_w(ph, 1, 1)

                def next_w(s, parity):
                    sp.wait_ge(c["proj_psum_ready"], ph.number_of(s, ("project", 3, 0), "project") + 1)
                    load_w(ph, s + 2, parity)

                def this_wo(s):
                    sp.wait_ge(c["y_psum_ready"], 2 * s)
                    load_wo(ph, s)

                next_w(0, 0)
                with sp.Fori(0, (STEPS - 4) // 2) as pair:
                    for s, parity in ((2 * pair + 1, 1), (2 * pair + 2, 0)):
                        next_w(s, parity)
                        this_wo(s)
                next_w(STEPS - 3, 1)
                for s in range(STEPS - 3, STEPS):
                    this_wo(s)
                sp.wait_ge(c["x_bank_empty"], ph.number_of(STEPS, ("output", 1, -1), "x") + 1)
            sp.wait_ge(experts_ready, 1)
            load_expert(0, 0)
            load_expert(1, 1)
            sp.wait_ge(scattered, 16 * TOPK * TILES)
            load_block(0, 0)
            load_block(1, 1)

            def next_block(j, par):
                sp.wait_ge(w13_ready, FT * (j - 1))
                sp.wait_ge(w2_ready, FT * (j - 1))
                load_expert(j, par)
                sp.wait_ge(block_turned, j - 1)
                load_block(j, par)
                store_result(j - 2, par)
            with sp.Fori(1, BLOCKS // 2) as pair:
                for par in range(2):
                    next_block(2 * pair + par, par)
            next_block(BLOCKS - 1, 0)
            store_result(BLOCKS - 2, 1)
            store_result(BLOCKS - 1, 0)
            sp.wait_ge(out_ready, 1)
            sp.dma_start(out.rearrange("(i p) h -> p i h", p=P), x[:, :, :]).then_inc(stored, 16)
            sp.wait_ge(stored, 16)

        @block.gpsimd
        def _(pool):
            pool.memset(identity[:, :], 0.0).then_inc(acc_cleared, 1)
            pool.memset(causal[:, :], 0.0).then_inc(acc_cleared, 1)
            pool.wait_ge(acc_cleared, 2)
            pool.affine_select(out=identity[:, :], in_=identity[:, :], compare_op=ALU.not_equal, fill=1.0,
                               base=0, pattern=[[-1, P]], channel_multiplier=1).then_inc(consts_ready, 1)
            pool.affine_select(out=causal[:, :], in_=causal[:, :], compare_op=ALU.is_ge, fill=MASKED,
                               base=0, pattern=[[-1, P]], channel_multiplier=1).then_inc(consts_ready, 1)
            pool.iota(iota_i[:, :, :], pattern=[[0, TILES], [1, E]], base=0, channel_multiplier=0)\
                .then_inc(consts_ready, 1)
            pool.iota(block_start_i[:, :, :], pattern=[[SLOTS, BLOCKS], [0, E]], base=0, channel_multiplier=0)\
                .then_inc(consts_ready, 1)
            pool.memset(acc[:, :, :], 0.0).then_inc(acc_cleared, 1)
            pool.memset(ones[:, :], 1.0).then_inc(acc_cleared, 1)
            pool.wait_ge(consts_ready, 4)
            pool.tensor_copy(identity_b[:, :], identity[:, :]).then_inc(small_ready, 1)
            pool.tensor_copy(causal_b[:, :], causal[:, :]).then_inc(small_ready, 1)
            pool.tensor_copy(iota_e[:, :, :], iota_i[:, :, :]).then_inc(small_ready, 1)
            pool.tensor_copy(block_start[:, :, :], block_start_i[:, :, :]).then_inc(small_ready, 1)
            pool.memset(ones_b[:, :], 1.0).then_inc(small_ready, 1)
            pool.wait_ge(small_ready, 5)
            pool.affine_select(out=earlier_b[:, :], in_=ones_b[:, :], compare_op=ALU.is_gt, fill=0.0,
                               base=0, pattern=[[1, P]], channel_multiplier=-1).then_inc(small_ready, 1)

            pool.wait_ge(acc_cleared, 4)
            pool.wait_ge(tables_loaded, 5 * 16)

            def attention(ph):
                c = ph.sems

                def take_projected(sp_, t, parity, i, x_number, number):
                    pool.wait_ge(c["x_bank_empty"], x_number + 1)
                    if ph.first:
                        pool.tensor_tensor(times_cos[:, i, :], projected[:, i, :], cosT[:, :], ALU.mult)\
                            .then_inc(c["cos_ready"], 1)
                        return
                    high_seen = number + 1
                    if t < T_K:
                        if not (isinstance(sp_, int) and sp_ == 0):
                            pool.wait_ge(c["scores_ready"], (sp_ - 1) * ph.units + (t + 1) * ph.group)
                        halves = (slice(0, D2), slice(D2, P))
                        for n in range(2):
                            part = projected[halves[n], i, :]
                            ins = pool.tensor_tensor(q_hl[halves[n], 2 * t + n, :], part,
                                                     ones[halves[n], 0:1].broadcast_to([D2, S]), ALU.mult)
                        ins.then_inc(c["high_ready"], 1)
                        pool.wait_ge(c["high_ready"], high_seen)
                        for n in range(2):
                            ins = pool.tensor_tensor(q_hl[halves[1 - n], 2 * t + n, :], projected[halves[n], i, :],
                                                     q_hl[halves[n], 2 * t + n, :].bitcast(F32), ALU.subtract)
                        ins.then_inc(c["q_ready"], 1)
                        return
                    buf = parity
                    for kv in range(2):
                        rows = slice(kv * D2, (kv + 1) * D2)
                        for half in range(2):
                            part = projected[rows, i, :]
                            ins = pool.tensor_tensor(k_hi[half * D2:(half + 1) * D2, buf, kv, :], part,
                                                     ones[rows, 0:1].broadcast_to([D2, S]), ALU.mult)
                    ins.then_inc(c["high_ready"], 1)
                    pool.wait_ge(c["high_ready"], high_seen)
                    for kv in range(2):
                        rows = slice(kv * D2, (kv + 1) * D2)
                        for half in range(2):
                            ins = pool.tensor_tensor(k_lo[half * D2:(half + 1) * D2, buf, kv, :],
                                                     projected[rows, i, :], k_hi[rows, buf, kv, :].bitcast(F32),
                                                     ALU.subtract)
                    ins.then_inc(c["k_ready"], 1)

                for n, t in enumerate(FIRST_TILES[:-1]):
                    take_projected(0, t, 0, n % 2, n, n)

                def slot(s, parity, u, of):
                    for e in ph.events(u, "rotate"):
                        if e[2] in of:
                            take_projected(s + e[2], e[1], (parity + e[2]) % 2, ph.parity_of(s, parity, e),
                                           ph.number_of(s, e, "x"), ph.number_of(s, e, "rotate"))
                steps(pool, slot, ph)
            attention(phases[0])
            attention(phases[1])

            pool.wait_ge(slots_ready, TOPK)
            pool.wait_ge(rows_cleared, 16 * len(range(0, BLOCKS * SLOTS // P * H, TILES * H)))
            for i in range(TILES):
                for n in range(TOPK):
                    pool.indirect_dma_start(out=slot_rows, out_offset=bass.IndirectOffsetOnAxis(
                        ap=slot_of[n][:, i:i + 1], axis=0), in_=htok[:, i, :], in_offset=None)\
                        .then_inc(scattered, 16)

            def split_w2(j, par):
                for f in range(FT):
                    pool.wait_ge(down_done, FT * j + f + 1)
                    pool.tensor_tensor(w2_hi[:, f, :], w2[par][:, f, :], ones[:, 0:1].broadcast_to([P, H]), ALU.mult)\
                        .then_inc(w2_high_ready, 1)
                    pool.wait_ge(w2_high_ready, FT * j + f + 1)
                    pool.tensor_tensor(w2_lo[:, f, :], w2[par][:, f, :], w2_hi[:, f, :].bitcast(F32), ALU.subtract)\
                        .then_inc(w2_ready, 1)

            for j in range(2):
                pool.wait_ge(weights_loaded[j], 48)
                split_w2(j, j)
            with pool.Fori(1, BLOCKS // 2) as pair:
                for par in range(2):
                    pool.wait_ge(weights_loaded[par], 48 * (pair + 1))
                    split_w2(2 * pair + par, par)
            pool.wait_ge(weights_loaded[0], 48 * (BLOCKS // 2 + 1))
            split_w2(BLOCKS - 1, 0)

            for par in range(2):
                pool.wait_ge(result_stored[par], 16 * (1 + (BLOCKS + 1 - par) // 2))
            for i in range(TILES):
                for n, dst in enumerate((htok[:, :, :], hT_rows)):
                    pool.indirect_dma_start(out=dst[:, i, :], out_offset=None, in_=slot_results,
                                            in_offset=bass.IndirectOffsetOnAxis(ap=slot_of[n][:, i:i + 1], axis=0))\
                        .then_inc(gathered[i // QT], 16)

        @block.tensor
        def _(pe):
            def turn_rows(norm):
                for b in range(B):
                    pe.wait_ge(rows_ready, B * norm + b + 1)
                    for k in range(KT):
                        for i in range(QT):
                            mm = pe.transpose(bank[KT * b + k][:, i * P:(i + 1) * P],
                                              htok[:, QT * b + i, k * P:(k + 1) * P], identity[:, :])
                        mm.then_inc(rows_turned, 1)
                pe.wait_ge(hT_ready, B * KT * (norm + 1))

            def attention(ph):
                c = ph.sems

                def project(sp_, t, parity, x_number):
                    if x_number is not None:
                        pe.wait_ge(c["x_bank_empty"], x_number)
                    if t == T_K or (isinstance(sp_, int) and sp_ == 0):
                        pe.wait_ge(c["w_odd_loaded" if parity else "w_even_loaded"], 16 * (sp_ // 2 + 1))
                    b = sp_ // G
                    for k in range(KT):
                        mm = pe.matmul(x_bank[:, :], w_qkv[:, parity, k, t * P:(t + 1) * P],
                                       hT[:, k, bass.ds(b * S, S)], start=(k == 0), stop=(k == KT - 1))
                    mm.then_inc(c["proj_psum_ready"], 1)

                def turn_v(x_number, o_number):
                    pe.wait_ge(c["x_bank_empty"], x_number + 1)
                    if o_number is not None:
                        pe.wait_ge(c["o_bank_empty"], o_number)
                    for i in range(QT):
                        mm = pe.transpose(o_bank[:, i * P:(i + 1) * P], vT[:, i * P:(i + 1) * P], identity[:, :])
                    mm.then_inc(c["v_psum_ready"], 1)

                def scores(s, parity, u):
                    h, q = u // QT, Q_ORDER[u % QT]
                    w = (q + 1) * P
                    dst = score_bank[u % N_SCORE]
                    if u % ph.group == 0:
                        pe.wait_ge(c["q_ready"], QTILES * s + u // ph.group + 1)
                    if u == 0:
                        pe.wait_ge(c["k_ready"], s + 1)
                    pe.wait_ge(c["probs_ready"], s * ph.units + u + 1)
                    if ph.first:
                        pe.matmul(dst[:, 0:w], qT[:, h, q * P:w], kT[:, parity, 0:w], start=True, stop=False)
                    else:
                        kv, wide = h // 4, max(w, 2 * P)
                        for n, part in enumerate((k_hi, k_lo)):
                            pe.matmul(dst[:, 0:wide], q_hl[:, h, q * P:w], part[:, parity, kv, 0:wide],
                                      start=(n == 0), stop=False)
                    pe.matmul(dst[:, q * P:w], identity_b[:, :], causal_b[:, :], start=False, stop=True)\
                        .then_inc(c["scores_ready"], 1)

                def turn(s, u):
                    q = Q_ORDER[u % QT]
                    pe.wait_ge(c["norm_ready"], s * ph.units + u + 1)
                    pe.wait_ge(c["pt_ready"], s * ph.units + u + 1)
                    for k in range(q + 1):
                        mm = pe.transpose(turn_bank[u % N_TURN][:, k * P:(k + 1) * P],
                                          probs[:, u % N_PROB, k * P:(k + 1) * P], identity[:, :])
                    mm.then_inc(c["pt_psum_ready"], 1)

                def values(s, parity, j, o_number):
                    pe.wait_ge(c["o_bank_empty"], o_number)
                    pe.wait_ge(c["pt_ready"], PT0 + s * ph.units + (j + 1) * ph.group)
                    for k in range(QT):
                        if ph.first:
                            mm = pe.matmul(o_bank[:, k * P:S], v[:, parity, k, :], probsT[:, j % 2, 0, k, k * P:S],
                                           start=(k == 0), stop=(k == QT - 1))
                        else:
                            kv = j // 2
                            for i in range(2):
                                mm = pe.matmul(o_bank[i * D2:(i + 1) * D2, k * P:S],
                                               v[:, parity, k, kv * D2:(kv + 1) * D2],
                                               probsT[:, j % 2, i, k, k * P:S], start=(k == 0), stop=(k == QT - 1))
                    mm.then_inc(c["o_psum_ready"], 1)

                def output(s, i, x_number, o_number):
                    if i == 0:
                        pe.wait_ge(c["wo_loaded"], 16 * (s + 1))
                        pe.wait_ge(c["o_bank_empty"], o_number + 1)
                    pe.wait_ge(c["x_bank_empty"], x_number)
                    for q in range(2 * i, 2 * i + 2):
                        for j in range(QTILES):
                            mm = pe.matmul(x_bank[:, (q % 2) * H:(q % 2 + 1) * H], oT[:, j, q * P:(q + 1) * P],
                                           w_o[:, j, :], start=(j == 0), stop=(j == QTILES - 1))
                    mm.then_inc(c["y_psum_ready"], 1)

                pe.sem_inc(c["pt_psum_ready"], PTPSUM0)
                pe.sem_inc(c["o_psum_ready"], OPSUM0)
                for n, t in enumerate(FIRST_TILES):
                    project(0, t, 0, n if n else None)
                turn_v(len(FIRST_TILES) - 1, None)

                def slot(s, parity, u, of):
                    if 0 in of and u < ph.units:
                        scores(s, parity, u)
                    back = unit_at(ph, s, u, LAG, of)
                    if back:
                        turn(*back)
                    for e in ph.slots.get(u, []):
                        kind, arg, d = e
                        if d not in of:
                            continue
                        if kind == "project":
                            project(s + d, arg, (parity + d) % 2, ph.number_of(s, e, "x"))
                        elif kind == "turn_v":
                            turn_v(ph.number_of(s, ("project", T_V, 1), "x"), ph.number_of(s, e, "o"))
                        elif kind == "values":
                            values(s + d, (parity + d) % 2, arg, ph.number_of(s, e, "o"))
                        else:
                            output(s + d, arg, ph.number_of(s, e, "x"),
                                   ph.number_of(s, ("values", QTILES - 1, -1), "o"))
                steps(pe, slot, ph)

            pe.wait_ge(consts_ready, 2)
            pe.wait_ge(small_ready, 2)
            for ph in phases:
                turn_rows(ph.number)
                attention(ph)

            turn_rows(2)
            for i in range(TILES):
                for k in range(KT):
                    mm = pe.matmul(router_bank[:, i * E:(i + 1) * E], hT[:, k, i * P:(i + 1) * P], gate_w[:, k, :],
                                   start=(k == 0), stop=(k == KT - 1))
            mm.then_inc(logits_ready, 1)
            pe.wait_ge(small_ready, 6)
            pe.wait_ge(chosen_ready, 1)
            pe.matmul(router_bank[:, 0:TILES * E], earlier_b[:, :], chosen_b[:, :], start=True, stop=True)
            pe.matmul(router_bank[:, TILES * E:2 * TILES * E], ones_b[:, :], chosen_b[:, :], start=True, stop=True)\
                .then_inc(ranks_ready, 1)

            pe.sem_inc(down_done, DOWN0)

            def turn_block(j, par):
                pe.wait_ge(block_loaded[par], 16 * (j // 2 + 1))
                if not (isinstance(j, int) and j == 0):
                    pe.wait_ge(block_T_ready, j)
                for k in range(KT):
                    for a in range(SA):
                        mm = pe.transpose(slot_bank[:, k * SLOTS + a * P:k * SLOTS + (a + 1) * P],
                                          slot_tok[:, par, a, k * P:(k + 1) * P], identity[:, :])
                mm.then_inc(block_turned, 1)

            def expert_block(j, par, last=False):
                def up(f):
                    dst = up_bank[f % N_UP]
                    cols = slice(f * P, (f + 1) * P)
                    pe.wait_ge(product_ready, FT * j + f + 1)
                    pe.wait_ge(w13_ready, FT * j + f + 1)
                    for n in range(2):
                        half = dst[:, n * SLOTS:(n + 1) * SLOTS]
                        for k in range(KT):
                            pe.matmul(half, w13_hi[:, n, k, cols], slot_hi[:, par, k, :], start=(k == 0), stop=False)
                            pe.matmul(half, w13_hi[:, n, k, cols], slot_lo[:, par, k, :], start=False, stop=False)
                            mm = pe.matmul(half, w13_lo[:, n, k, cols], slot_hi[:, par, k, :],
                                           start=False, stop=(k == KT - 1))
                    mm.then_inc(up_ready, 1)

                def down(f):
                    if f == 0:
                        pe.wait_ge(result_ready, j + 1)
                    pe.wait_ge(w2_ready, FT * j + f + 1)
                    pe.wait_ge(gated_ready, FT * j + f + 1)
                    i = f % N_GATED
                    for a in range(SA):
                        half, rows = down_bank[par][:, a * H:(a + 1) * H], slice(a * P, (a + 1) * P)
                        pe.matmul(half, gated_hi[:, i, rows], w2_hi[:, f, :], start=(f == 0 and a == 0), stop=False,
                                  skip_group_check=True)
                        pe.matmul(half, gated_hi[:, i, rows], w2_lo[:, f, :], start=False, stop=False,
                                  skip_group_check=True)
                        mm = pe.matmul(half, gated_lo[:, i, rows], w2_hi[:, f, :], start=False, stop=(f == FT - 1),
                                       skip_group_check=True)
                    mm.then_inc(down_done, 1)

                pe.wait_ge(block_T_ready, j + 1)
                for f in range(FT + DOWN_LAG):
                    if f < FT:
                        up(f)
                    if f == FT - 1 and not last:
                        turn_block(j + 1, 1 - par)
                    if f >= DOWN_LAG:
                        down(f - DOWN_LAG)

            turn_block(0, 0)
            with pe.Fori(0, BLOCKS // 2) as pair:
                for par in range(2):
                    expert_block(2 * pair + par, par)
            expert_block(BLOCKS - 1, 0, True)

        @block.scalar
        def _(act):
            roots = [0]

            def root_of_square():
                roots[0] += 1
                act.wait_ge(root_asked, roots[0])
                act.activation(root[:, :], square[:, :], ACT.Sqrt).then_inc(root_ready, 1)

            def take_rows(norm):
                if norm == 0:
                    act.wait_ge(tables_loaded, 5 * 16)
                for b in range(B):
                    for k in range(KT):
                        act.wait_ge(rows_turned, B * KT * norm + KT * b + k + 1)
                        act.activation(hT[:, k, b * S:(b + 1) * S], bank[KT * b + k][:, :], ACT.Copy,
                                       scale=ln_w[:, norm, k:k + 1]).then_inc(hT_ready, 1)

            def attention(ph):
                c = ph.sems
                act.sem_inc(c["probs_ready"], PROBS0)
                act.sem_inc(c["pt_ready"], PT0)

                def take_projection(sp_, t, i, number, before):
                    act.wait_ge(c["proj_psum_ready"], number + 1)
                    if t == T_V:
                        dst = vT[:, :]
                        before = ("v_psum_ready", sp_)
                    else:
                        dst = projected[:, i, :]
                    if before[0] and not (isinstance(before[1], int) and before[1] == 0):
                        act.wait_ge(c[before[0]], before[1])
                    if ph.first:
                        ins = act.activation(dst, x_bank[:, :], ACT.Identity, bias=bias[:, bass.ds(sp_ % G, 1), t])
                    elif t < T_K:
                        ins = act.activation(dst, x_bank[:, :], ACT.Copy, scale=D2 ** -0.5)
                    else:
                        ins = act.activation(dst, x_bank[:, :], ACT.Copy)
                    ins.then_inc(c["x_bank_empty"], 1)

                def take_v(sp_, parity):
                    act.wait_ge(c["v_psum_ready"], sp_ + 1)
                    act.activation(v[:, parity, :, :], o_bank[:, :].rearrange("p (i d) -> p i d", i=QT), ACT.Copy)\
                        .then_inc(c["o_bank_empty"], 1)

                def exponentials(s, u):
                    w = (Q_ORDER[u % QT] + 1) * P
                    i = u % N_PROB
                    act.wait_ge(c["max_ready"], s * ph.units + u + 1)
                    act.wait_ge(c["pt_psum_ready"], s * ph.units + u + 1)
                    act.activation(probs[:, i, 0:w], score_bank[u % N_SCORE][:, 0:w], ACT.Exp,
                                   bias=negmax[:, i:i + 1], accum_out=rowsum[:, i:i + 1])\
                        .then_inc(c["probs_ready"], 1)

                def take_turned(s, u):
                    q = Q_ORDER[u % QT]
                    j = u // ph.group
                    i = 0 if ph.first else u // QT % 2
                    act.wait_ge(c["pt_psum_ready"], PTPSUM0 + s * ph.units + u + 1)
                    if u % ph.group == 0:
                        act.wait_ge(c["o_psum_ready"], QTILES * s + j + 1)
                    act.activation(probsT[:, j % 2, i, 0:q + 1, q * P:(q + 1) * P],
                                   turn_bank[u % N_TURN][:, 0:(q + 1) * P].rearrange("p (k n) -> p k n", n=P),
                                   ACT.Copy).then_inc(c["pt_ready"], 1)

                for n, t in enumerate(FIRST_TILES):
                    before = ("k_ready", 1) if n == 2 else ("q_ready", max(n - 2, 0))
                    take_projection(0, t, n % 2, n, before)
                take_v(0, 0)

                def slot(s, parity, u, of):
                    if 0 in of and u < ph.units:
                        exponentials(s, u)
                    back = unit_at(ph, s, u, LAG, of)
                    if back:
                        take_turned(*back)
                    for e in ph.slots.get(u, []):
                        kind, arg, d = e
                        if d not in of:
                            continue
                        if kind == "project" and arg == T_V:
                            take_projection(s + d, arg, None, ph.number_of(s, e, "project"), None)
                        elif kind == "project":
                            take_projection(s + d, arg, ph.parity_of(s, parity, e), ph.number_of(s, e, "project"),
                                            ph.two_before(s, e))
                        elif kind == "turn_v":
                            take_v(s + d, (parity + d) % 2)
                steps(act, slot, ph)

            root_of_square()
            root_of_square()
            take_rows(0)
            attention(phases[0])
            for _ in range(3):
                root_of_square()
            take_rows(1)
            attention(phases[1])
            root_of_square()
            take_rows(2)
            act.wait_ge(e_shifted, 1)
            act.activation(e_prob[:, :, :], pick[:, :, :], ACT.Exp).then_inc(e_exp_ready, 1)

            def take_block(j, par):
                act.wait_ge(block_turned, j + 1)
                for k in range(KT):
                    ins = act.activation(slot_hi[:, par, k, :], slot_bank[:, k * SLOTS:(k + 1) * SLOTS], ACT.Copy,
                                         scale=ln_w[:, 2, k:k + 1])
                ins.then_inc(block_high_ready, 1)

            def split_high(j, par, f):
                cols = slice(f * P, (f + 1) * P)
                if f == 0:
                    act.wait_ge(weights_loaded[par], 48 * (j // 2 + 1))
                act.wait_ge(down_done, FT * j + f + 1)
                act.activation(w13_hi[:, :, :, cols].rearrange("p n k c -> p (n k) c"),
                               w13[par][:, :, :, cols].rearrange("p n k c -> p (n k) c"), ACT.Copy)\
                    .then_inc(w13_high_ready, 1)

            def expert_block(j, par, last=False):
                for f in range(FT + SPLIT_LAG):
                    if f < FT:
                        act.wait_ge(up_ready, FT * j + f + 1)
                        act.activation(rectified[:, f % N_UP, :], up_bank[f % N_UP][:, 0:SLOTS], ACT.Relu)\
                            .then_inc(relu_ready, 1)
                    if 1 <= f <= FT:
                        g = f - 1
                        act.wait_ge(product_ready, PRODUCT0 + FT * j + g + 1)
                        act.activation(gated_hi[:, g % N_GATED, :], gated[:, g % N_GATED, :], ACT.Copy)\
                            .then_inc(gated_high_ready, 1)
                    if f == FT and not last:
                        take_block(j + 1, 1 - par)
                    if f >= SPLIT_LAG and not last:
                        split_high(j + 1, 1 - par, f - SPLIT_LAG)

            for f in range(FT):
                split_high(0, 0, f)
            take_block(0, 0)
            with act.Fori(0, BLOCKS // 2) as pair:
                for par in range(2):
                    expert_block(2 * pair + par, par)
            expert_block(BLOCKS - 1, 0, True)
            root_of_square()

        @block.vector
        def _(dve):
            count = [0, 0]

            def link(ins):
                count[0] += 1
                ins.then_inc(dve_step, 1)
                dve.wait_ge(dve_step, count[0])

            def moments(src):
                for i in range(TILES):
                    ins = dve.bn_stats(stats[:, i, :], src[:, i, :])
                link(ins)
                for i in range(TILES):
                    ins = dve.bn_aggr(mv[:, i, :], stats[:, i, :])
                link(ins)
            mean, var = mv[:, :, 0], mv[:, :, 1]

            def inverse_root(dst, src, eps):
                count[1] += 1
                dve.tensor_scalar(square[:, :], src, eps, None, ALU.add).then_inc(root_asked, 1)
                dve.wait_ge(root_ready, count[1])
                link(dve.reciprocal(dst[:, :], root[:, :]))

            def minus_mean_times(inv):
                link(dve.scalar_tensor_tensor(out=shift[:, :], in0=mean, scalar=-1.0, in1=inv[:, :],
                                              op0=ALU.mult, op1=ALU.mult))

            def scaled(dst, src, factor, sum_sem=None):
                for i in range(TILES):
                    ins = dve.tensor_scalar(dst[:, i, :], src[:, i, :], factor[:, i:i + 1], shift[:, i:i + 1],
                                            ALU.mult, ALU.add)
                    if sum_sem is not None and i % QT == QT - 1:
                        ins.then_inc(sum_sem, 1)
                if sum_sem is None:
                    link(ins)

            def times(dst, src, factor):
                for i in range(TILES):
                    ins = dve.tensor_scalar(dst[:, i, :], src[:, i, :], factor[:, i:i + 1], None, ALU.mult)
                    if i % QT == QT - 1:
                        ins.then_inc(rows_ready, 1)

            def norm_of_norm(eps):
                moments(x)
                inverse_root(inv1, var, LN_EPS)
                link(dve.tensor_tensor(scale[:, :], inv1[:, :], inv1[:, :], ALU.mult))
                link(dve.tensor_tensor(scale[:, :], scale[:, :], var, ALU.mult))
                inverse_root(inv2, scale[:, :], eps)

            def add_norm_of_acc():
                moments(acc)
                inverse_root(inv1, var, LN_EPS)
                minus_mean_times(inv1)
                scaled(acc, acc, inv1)
                return dve.tensor_tensor(x[:, :, :], x[:, :, :], acc[:, :, :], ALU.add)

            def attention(ph):
                c = ph.sems

                def rotate(sp_, t, parity, i, x_number, number):
                    queries = t < T_K
                    dve.wait_ge(c["x_bank_empty"], x_number + 1)
                    dve.tensor_tensor(times_sin[0:D1 // 2, i, :], projected[D1 // 2:D1, i, :],
                                      sinT[D1 // 2:D1, :], ALU.mult)
                    dve.tensor_tensor(times_sin[D1 // 2:D1, i, :], projected[0:D1 // 2, i, :],
                                      sinT[0:D1 // 2, :], ALU.mult).then_inc(c["sin_ready"], 1)
                    dve.wait_ge(c["sin_ready"], number + 1)
                    dve.wait_ge(c["cos_ready"], number + 1)
                    if queries and not (isinstance(sp_, int) and sp_ == 0):
                        dve.wait_ge(c["scores_ready"], (sp_ - 1) * ph.units + (t + 1) * ph.group)
                    dst = qT[:, t, :] if queries else kT[:, parity, :]
                    dve.tensor_tensor(dst, times_cos[:, i, :], times_sin[:, i, :], ALU.add)\
                        .then_inc(c["q_ready" if queries else "k_ready"], 1)

                def maximum(s, u):
                    i = u % N_PROB
                    dve.wait_ge(c["scores_ready"], s * ph.units + u + 1)
                    dve.tensor_reduce(negmax[:, i:i + 1], score_bank[u % N_SCORE][:, 0:(Q_ORDER[u % QT] + 1) * P], AX_X,
                                      ALU.max, negate=True).then_inc(c["max_ready"], 1)

                def invert(s, u):
                    i = u % N_PROB
                    dve.wait_ge(c["probs_ready"], PROBS0 + s * ph.units + u + 1)
                    dve.reciprocal(rinv[:, i:i + 1], rowsum[:, i:i + 1]).then_inc(c["rinv_ready"], 1)

                def normalise(s, u):
                    i = u % N_PROB
                    w = (Q_ORDER[u % QT] + 1) * P
                    dve.wait_ge(c["rinv_ready"], s * ph.units + u + 1)
                    dve.tensor_scalar(probs[:, i, 0:w], probs[:, i, 0:w], rinv[:, i:i + 1], None, ALU.mult)\
                        .then_inc(c["norm_ready"], 1)

                def take_values(s, j):
                    dve.wait_ge(c["o_psum_ready"], OPSUM0 + QTILES * s + j + 1)
                    if j == 0 and not (isinstance(s, int) and s == 0):
                        dve.wait_ge(c["y_psum_ready"], 2 * s)
                    dve.tensor_copy(oT[:, j, :], o_bank[:, :]).then_inc(c["o_bank_empty"], 1)

                def add_output(s, i, x_number):
                    dve.wait_ge(c["y_psum_ready"], 2 * s + i + 1)
                    dve.wait_ge(c["x_bank_empty"], x_number)
                    b = s // G
                    dst = acc[:, bass.ds(b * QT + 2 * i, 2), :]
                    dve.tensor_tensor(dst, dst, x_bank[:, :].rearrange("p (i h) -> p i h", i=2), ALU.add)\
                        .then_inc(c["x_bank_empty"], 1)

                if ph.first:
                    for n, t in enumerate(FIRST_TILES[:-1]):
                        rotate(0, t, 0, n % 2, n, n)

                def slot(s, parity, u, of):
                    back = unit_at(ph, s, u, 2, of)
                    if back:
                        invert(*back)
                    if 0 in of and u < ph.units:
                        maximum(s, u)
                    if back:
                        normalise(*back)
                    if ph.first and u >= 1:
                        for e in ph.events(u - 1, "rotate"):
                            if e[2] in of:
                                rotate(s + e[2], e[1], (parity + e[2]) % 2, ph.parity_of(s, parity, e),
                                       ph.number_of(s, e, "x"), ph.number_of(s, e, "rotate"))
                    for e in ph.slots.get(u, []):
                        kind, arg, d = e
                        if d not in of:
                            continue
                        if kind == "values":
                            take_values(s + d, arg)
                        elif kind == "output":
                            add_output(s + d, arg, ph.number_of(s, e, "x"))
                if ph.first:
                    dve.wait_ge(acc_cleared, 3)
                    dve.wait_ge(rows_cleared, 16 * len(range(0, BLOCKS * SLOTS // P * H, TILES * H)))
                steps(dve, slot, ph)
                dve.wait_ge(c["x_bank_empty"], ph.number_of(STEPS, ("output", 1, -1), "x") + 1)

            dve.wait_ge(x_loaded, 16)
            norm_of_norm(RMS_A_EPS)
            link(dve.tensor_tensor(scale[:, :], inv1[:, :], inv2[:, :], ALU.mult))
            minus_mean_times(scale)
            scaled(htok, x, scale, rows_ready)
            attention(phases[0])

            link(add_norm_of_acc())
            norm_of_norm(RMS_B_EPS)
            minus_mean_times(inv1)
            scaled(acc, x, inv1)
            times(htok, acc, inv2)
            attention(phases[1])

            moments(acc)
            link(dve.tensor_tensor(scale[:, :], mean, mean, ALU.mult))
            link(dve.tensor_tensor(scale[:, :], scale[:, :], var, ALU.add))
            inverse_root(inv1, scale[:, :], RMS_B_EPS)
            times(htok, acc, inv1)

            dve.sem_inc(product_ready, PRODUCT0)
            dve.sem_inc(result_ready, RESULT0)
            for par in range(2):
                dve.sem_inc(result_stored[par], 16)
            dve.wait_ge(logits_ready, 1)
            logits = router_bank[:, 0:TILES * E].rearrange("p (i e) -> p i e", e=E)
            link(dve.tensor_copy(pick[:, :, :], logits))
            link(dve.tensor_reduce(e_max[:, :], pick[:, :, :], AX_X, ALU.max))
            link(dve.tensor_tensor(pick[:, :, :], pick[:, :, :],
                                   e_max[:, :].unsqueeze(2).broadcast_to([P, TILES, E]), ALU.subtract))
            dve.sem_inc(e_shifted, 1)
            dve.wait_ge(e_exp_ready, 1)
            link(dve.tensor_reduce(e_sum[:, :], e_prob[:, :, :], AX_X, ALU.add))
            link(dve.reciprocal(e_sum[:, :], e_sum[:, :]))
            link(dve.tensor_tensor(e_prob[:, :, :], e_prob[:, :, :],
                                   e_sum[:, :].unsqueeze(2).broadcast_to([P, TILES, E]), ALU.mult))
            for i in range(TILES):
                ins = dve.max(e_top[:, i, :], e_prob[:, i, :])
            link(ins)
            for i in range(TILES):
                ins = dve.max_index(e_topi[:, i, :], e_top[:, i, :], e_prob[:, i, :])
            link(ins)
            link(dve.tensor_copy(e_topf[:, :, :], e_topi[:, :, :]))
            dve.wait_ge(small_ready, 6)
            for n in range(TOPK):
                ins = dve.tensor_tensor(choice[n][:, :, :], iota_e[:, :, :],
                                        e_topf[:, :, n:n + 1].broadcast_to([P, TILES, E]), ALU.is_equal)
            link(ins)
            dve.tensor_tensor(chosen_b[:, :], choice[0][:, :, :].rearrange("p i e -> p (i e)"),
                              choice[1][:, :, :].rearrange("p i e -> p (i e)"), ALU.add).then_inc(chosen_ready, 1)
            link(dve.tensor_tensor(e_sum[:, :], e_top[:, :, 0], e_top[:, :, 1], ALU.add))
            link(dve.reciprocal(e_sum[:, :], e_sum[:, :]))
            for n in range(TOPK):
                ins = dve.tensor_tensor(share[n][:, :], e_top[:, :, n], e_sum[:, :], ALU.mult)
            link(ins)
            link(dve.memset(run[:, 0, :], 0.0))
            link(dve.memset(first_slot[:, 0:1], 0.0))

            dve.wait_ge(ranks_ready, 1)
            for i in range(TILES):
                link(dve.tensor_tensor(run[:, i + 1, :], run[:, i, :],
                                       router_bank[:, (TILES + i) * E:(TILES + i + 1) * E], ALU.add))
            link(dve.tensor_scalar(whole[:, :], run[:, TILES, :], float(SLOTS - 1), None, ALU.add))
            link(dve.tensor_copy(whole_i[:, :], whole[:, :]))
            link(dve.tensor_scalar(whole_i[:, :], whole_i[:, :], -SLOTS, None, ALU.bitwise_and))
            link(dve.tensor_copy(whole[:, :], whole_i[:, :]))
            for e in range(E):
                link(dve.tensor_tensor(first_slot[:, e + 1:e + 2], first_slot[:, e:e + 1], whole[:, e:e + 1], ALU.add))
            link(dve.tensor_tensor(passed[:, :, :], block_start[:, :, :],
                                   first_slot[:, 1:E + 1].unsqueeze(1).broadcast_to([P, BLOCKS, E]), ALU.is_ge))
            link(dve.tensor_reduce(block_expert_f[:, :], passed[:, :, :], AX_X, ALU.add))
            link(dve.tensor_scalar(block_expert_f[:, :], block_expert_f[:, :], float(E - 1), None, ALU.min))
            dve.tensor_copy(block_expert[:, :], block_expert_f[:, :]).then_inc(experts_ready, 1)
            link(dve.tensor_tensor(place[:, :, :], logits, run[:, 0:TILES, :], ALU.add))
            link(dve.tensor_tensor(place[:, :, :], place[:, :, :],
                                   first_slot[:, 0:E].unsqueeze(1).broadcast_to([P, TILES, E]), ALU.add))
            for n in range(TOPK):
                link(dve.tensor_tensor(pick[:, :, :], place[:, :, :], choice[n][:, :, :], ALU.mult))
                link(dve.tensor_reduce(slot_f[:, :], pick[:, :, :], AX_X, ALU.add))
                ins = dve.tensor_copy(slot_of[n][:, :], slot_f[:, :])
                ins.then_inc(slots_ready, 1)
                dve.wait_ge(slots_ready, n + 1)

            def take_block(j, par):
                dve.wait_ge(block_high_ready, j + 1)
                for k in range(KT):
                    ins = dve.scalar_tensor_tensor(out=slot_lo[:, par, k, :], in0=slot_bank[:, k * SLOTS:(k + 1) * SLOTS],
                                                   scalar=ln_w[:, 2, k:k + 1], in1=slot_hi[:, par, k, :].bitcast(F32),
                                                   op0=ALU.mult, op1=ALU.subtract)
                ins.then_inc(block_T_ready, 1)

            def split_low(j, par, f):
                cols = slice(f * P, (f + 1) * P)
                dve.wait_ge(w13_high_ready, FT * j + f + 1)
                dve.tensor_tensor(w13_lo[:, :, :, cols].rearrange("p n k c -> p (n k) c"),
                                  w13[par][:, :, :, cols].rearrange("p n k c -> p (n k) c"),
                                  w13_hi[:, :, :, cols].rearrange("p n k c -> p (n k) c").bitcast(F32), ALU.subtract)\
                    .then_inc(w13_ready, 1)

            def expert_block(j, par, last=False):
                for f in range(FT + SPLIT_LAG):
                    i, g = f % N_GATED, f - 1
                    if f < FT:
                        dve.wait_ge(relu_ready, FT * j + f + 1)
                        dve.wait_ge(down_done, DOWN0 - N_GATED + FT * j + f + 1)
                        dve.tensor_tensor(gated[:, i, :], up_bank[f % N_UP][:, SLOTS:2 * SLOTS],
                                          rectified[:, f % N_UP, :], ALU.mult).then_inc(product_ready, 1)
                    if 1 <= f <= FT:
                        i = g % N_GATED
                        dve.wait_ge(gated_high_ready, FT * j + g + 1)
                        dve.tensor_tensor(gated_lo[:, i, :], gated[:, i, :], gated_hi[:, i, :].bitcast(F32),
                                          ALU.subtract).then_inc(gated_ready, 1)
                    if f == FT and not last:
                        take_block(j + 1, 1 - par)
                    if f >= SPLIT_LAG and not last:
                        split_low(j + 1, 1 - par, f - SPLIT_LAG)
                dve.wait_ge(down_done, DOWN0 + FT * (j + 1))
                dve.wait_ge(result_stored[par], 16 * (j // 2 + 1))
                dve.tensor_copy(result[:, par, :, :], down_bank[par][:, :].rearrange("p (a h) -> p a h", a=SA))\
                    .then_inc(result_ready, 1)

            for f in range(FT):
                split_low(0, 0, f)
            take_block(0, 0)
            with dve.Fori(0, BLOCKS // 2) as pair:
                for par in range(2):
                    expert_block(2 * pair + par, par)
            expert_block(BLOCKS - 1, 0, True)

            for b in range(B):
                dve.wait_ge(gathered[b], 16 * TOPK * QT)
                for n, rows in enumerate((htok[:, :, :], hT_rows)):
                    for i in range(b * QT, (b + 1) * QT):
                        ins = dve.scalar_tensor_tensor(out=acc[:, i, :], in0=rows[:, i, :], scalar=share[n][:, i:i + 1],
                                                       in1=acc[:, i, :], op0=ALU.mult, op1=ALU.add)
                    link(ins)
            add_norm_of_acc().then_inc(out_ready, 1)

        del block


def kernel(**inputs):
    import numpy as np
    import concourse.bacc as bacc
    from concourse.bass_utils import run_bass_kernel_spmd

    a = {k: np.asarray(v) for k, v in inputs.items()}

    def tiles(n, count):
        return a[n].reshape(G, count, H).transpose(0, 2, 1)

    def columns(n, count):
        return a[n].reshape(H, G, count).transpose(1, 0, 2)

    inv_freq = (np.float32(1.0) / np.float32(10000.0) ** (np.arange(0, D1, 2, dtype=np.float32) / np.float32(D1)))
    angle = (np.arange(S, dtype=np.float32)[:, None] * inv_freq.astype(np.float32)).T
    half_scale = float(D1) ** -0.25
    cos, sin = np.cos(angle.astype(np.float64)) * half_scale, np.sin(angle.astype(np.float64)) * half_scale
    arrays = {
        "x_in": a["L0_attn_x"].reshape(T, H),
        "cos_in": np.concatenate([cos, cos]).astype(np.float32),
        "sin_in": np.concatenate([sin, -sin]).astype(np.float32),
        "wa_in": np.concatenate([tiles("L0_attn_q_project", QROWS), tiles("L0_attn_k_project", P),
                                 tiles("L0_attn_v_project", P)], axis=2).reshape(G * H, WROWS),
        "ba_in": np.concatenate([a["L0_attn_q_bias"].reshape(G, QTILES, P), a["L0_attn_k_bias"].reshape(G, 1, P),
                                 a["L0_attn_v_bias"].reshape(G, 1, P)], axis=1).transpose(2, 0, 1),
        "oa_in": a["L0_attn_o_project"].T,
        "wb_in": np.concatenate([columns("L0_ffn_wq", QROWS), columns("L0_ffn_wk", P),
                                 columns("L0_ffn_wv", P)], axis=2).reshape(G * H, WROWS),
        "ob_in": a["L0_ffn_wo"],
        "ln_in": np.stack([a["L0_attn_ln_weight"], a["L0_ffn_ln1_w"], a["L0_ffn_ln2_w"]])
        .reshape(3, KT, P).transpose(2, 0, 1),
        "gate_in": a["L0_ffn_gate_w"],
        "w1_in": a["L0_ffn_w1"].reshape(E * H, F),
        "w2_in": a["L0_ffn_w2"].reshape(E * F, H),
        "w3_in": a["L0_ffn_w3"].reshape(E * H, F),
    }
    arrays = {k: np.ascontiguousarray(v) for k, v in arrays.items()}
    nc = bacc.Bacc("TRN2", target_bir_lowering=False, num_devices=1)
    args = {k: nc.dram_tensor(f"{k}_dram", v.shape, mybir.dt.from_np(v.dtype), kind="ExternalInput").ap()
            for k, v in arrays.items()}
    result = nc.dram_tensor("result_dram", (T, H), F32, kind="ExternalOutput").ap()
    program(nc, out=result, **args)
    r = run_bass_kernel_spmd(nc, [{f"{k}_dram": v for k, v in arrays.items()}], core_ids=[0])
    return r.results[0]["result_dram"].reshape(B, S, H)
```

```python
from contextlib import ExitStack

import concourse.bass as bass
from concourse import mybir

F32 = mybir.dt.float32
F32R = mybir.dt.float32r
BF16 = mybir.dt.bfloat16
I32 = mybir.dt.int32
U32 = mybir.dt.uint32
ALU = mybir.AluOpType
ACT = mybir.ActivationFunctionType
AX_X = mybir.AxisListType.X

P = 128
B, S, H = 4, 512, 256
T = B * S
TILES = T // P
KT = H // P
QT = S // P
G = 4
QROWS = 512
QTILES = QROWS // P
WROWS = QROWS + 2 * P
PROJ = WROWS // P
T_K, T_V = QTILES, QTILES + 1
STEPS = B * G
D1, D2 = 128, 64
E, F = 8, 1024
FT = F // P
TOPK = 2
SLOTS = 256
BLOCKS = (TOPK * T + E * (SLOTS - 1)) // SLOTS
SA = SLOTS // P
LN_EPS = 1e-5
RMS_A_EPS = 1e-6
RMS_B_EPS = 1e-5
MASKED = -1e30
Q_ORDER = (0, 1, 3, 2)
LAG = 6
VALUES_LAG = 2
N_SCORE = 4
N_PROB = 8
N_TURN = 2
DOWN_LAG = 3
N_UP = 4
SPLIT_LAG = 4
N_GATED = 4


def program(nc, x_in, cos_in, sin_in, wa_in, ba_in, oa_in,
            wb_in, ob_in, ln_in, gate_in, w1_in, w2_in, w3_in, out):
    with ExitStack() as ctx:
        def sb(name, shape, dt=F32, stack=ctx):
            return stack.enter_context(nc.sbuf_tensor(name, shape, dt))

        def sem(name):
            return ctx.enter_context(nc.semaphore(name))

        bank = [ctx.enter_context(nc.psum_tensor(f"bank{i}", [P, 512], F32)) for i in range(8)]
        score_bank, turn_bank, o_bank, x_bank = bank[0:4], bank[4:6], bank[6], bank[7]
        up_bank, down_bank, router_bank, slot_bank = bank[0:4], bank[4:6], bank[6], bank[7]

        slot_rows = nc.dram_tensor("slot_rows", (BLOCKS * SLOTS, H), F32).ap()
        slot_results = nc.dram_tensor("slot_results", (BLOCKS * SLOTS, H), F32).ap()

        x = sb("x", [P, TILES, H])
        acc = sb("acc", [P, TILES, H])
        second_keys = ExitStack()
        k_hi = sb("k_hi", [P, 2, 2, S], F32R, stack=second_keys)
        k_lo = sb("k_lo", [P, 2, 2, S], F32R, stack=second_keys)
        second_keys.close()
        first_keys = ExitStack()
        qT = sb("qT", [P, QTILES, S], stack=first_keys)
        kT = sb("kT", [P, 2, S], stack=first_keys)
        times_cos = sb("times_cos", [P, 2, S], stack=first_keys)
        first_keys.close()
        htok = sb("htok", [P, TILES, H])
        split_rows = ExitStack()
        hT_hi = sb("hT_hi", [P, KT, T], F32R, stack=split_rows)
        hT_lo = sb("hT_lo", [P, KT, T], F32R, stack=split_rows)
        split_rows.close()
        hT = sb("hT", [P, KT, T])
        gated = sb("gated", [P, N_GATED, SLOTS])
        gated_hi = sb("gated_hi", [P, N_GATED, SLOTS], F32R)
        gated_lo = sb("gated_lo", [P, N_GATED, SLOTS], F32R)
        rectified = sb("rectified", [P, N_UP, SLOTS])
        identity = sb("identity", [P, P])
        causal = sb("causal", [P, P])
        identity_b = sb("identity_b", [P, P], BF16)
        causal_b = sb("causal_b", [P, P], BF16)
        iota_i = sb("iota_i", [P, TILES, E], I32)
        iota_e = sb("iota_e", [P, TILES, E])
        ln_w = sb("ln_w", [P, 3, KT])
        gate_w = sb("gate_w", [P, KT, E])
        ones = sb("ones", [P, 1])
        stats = sb("stats", [P, TILES, 6])
        mv = sb("mv", [P, TILES, 2])
        square = sb("square", [P, TILES])
        root = sb("root", [P, TILES])
        inv1 = sb("inv1", [P, TILES])
        inv2 = sb("inv2", [P, TILES])
        scale = sb("scale", [P, TILES])
        shift = sb("shift", [P, TILES])
        norm_shift = sb("norm_shift", [P, TILES])
        earlier_b = sb("earlier_b", [P, P], BF16)
        ones_b = sb("ones_b", [P, P], BF16)
        block_start_i = sb("block_start_i", [P, BLOCKS, E], I32)
        block_start = sb("block_start", [P, BLOCKS, E])

        both, first_only, second_only = ExitStack(), ExitStack(), ExitStack()
        bias = sb("bias", [P, G, PROJ], stack=both)
        w_qkv = sb("w_qkv", [P, KT, WROWS], stack=both)
        w_hi = sb("w_hi", [P, KT, WROWS], F32R, stack=both)
        w_lo = sb("w_lo", [P, KT, WROWS], F32R, stack=both)
        w_o = sb("w_o", [P, QTILES, H], stack=both)
        wo_hi = sb("wo_hi", [P, QTILES, H], F32R, stack=both)
        wo_lo = sb("wo_lo", [P, QTILES, H], F32R, stack=both)
        projected = sb("projected", [P, 2, S], stack=both)
        vT = sb("vT", [P, S], stack=both)
        v = sb("v", [P, 2, QT, P], stack=both)
        probs = sb("probs", [P, N_PROB, S], stack=both)
        probsT = sb("probsT", [P, 2, 2, QT, S], stack=both)
        oT_hi = sb("oT_hi", [P, QTILES, S], F32R, stack=both)
        oT_lo = sb("oT_lo", [P, QTILES, S], F32R, stack=both)
        negmax = sb("negmax", [P, N_PROB], stack=both)
        rowsum = sb("rowsum", [P, N_PROB], stack=both)
        rinv = sb("rinv", [P, N_PROB], stack=both)
        cosT = sb("cosT", [P, S], stack=first_only)
        sinT = sb("sinT", [P, S], stack=first_only)
        times_sin = sb("times_sin", [P, 2, S], stack=first_only)
        first_only.close()
        q_hl = sb("q_hl", [P, 2 * QTILES, S], F32R, stack=second_only)
        second_only.close()
        both.close()
        e_max = sb("e_max", [P, TILES])
        e_sum = sb("e_sum", [P, TILES])
        e_prob = sb("e_prob", [P, TILES, E])
        e_top = sb("e_top", [P, TILES, E])
        e_topi = sb("e_topi", [P, TILES, E], U32)
        e_topf = sb("e_topf", [P, TILES, E])
        pick = sb("pick", [P, TILES, E])
        choice = [sb(f"choice{n}", [P, TILES, E]) for n in range(TOPK)]
        share = [sb(f"share{n}", [P, TILES]) for n in range(TOPK)]
        chosen_b = sb("chosen_b", [P, TILES * E], BF16)
        run = sb("run", [P, TILES + 1, E])
        whole_i = sb("whole_i", [P, E], I32)
        whole = sb("whole", [P, E])
        first_slot = sb("first_slot", [P, E + 1])
        place = sb("place", [P, TILES, E])
        slot_f = sb("slot_f", [P, TILES])
        slot_of = [sb(f"slot_of{n}", [P, TILES], U32) for n in range(TOPK)]
        passed = sb("passed", [P, BLOCKS, E])
        block_expert_f = sb("block_expert_f", [P, BLOCKS])
        block_expert = sb("block_expert", [P, BLOCKS], I32)
        w13 = [sb(f"w13_{name}", [P, 2, KT, F]) for name in ("even", "odd")]
        w2 = [sb(f"w2_{name}", [P, FT, H]) for name in ("even", "odd")]
        w13_hi = sb("w13_hi", [P, 2, KT, F], F32R)
        w13_lo = sb("w13_lo", [P, 2, KT, F], F32R)
        w2_hi = sb("w2_hi", [P, FT, H], F32R)
        w2_lo = sb("w2_lo", [P, FT, H], F32R)
        slot_tok = sb("slot_tok", [P, 2, SA, H])
        slot_hi = sb("slot_hi", [P, 2, KT, SLOTS], F32R)
        slot_lo = sb("slot_lo", [P, 2, KT, SLOTS], F32R)
        result = sb("result", [P, 2, SA, H])

        hT_rows = hT[:, :, :].rearrange("p k (i h) -> p (k i) h", h=H)

        x_loaded = sem("x_loaded")
        tables_loaded = sem("tables_loaded")
        consts_ready = sem("consts_ready")
        small_ready = sem("small_ready")
        acc_cleared = sem("acc_cleared")
        dve_step = sem("dve_step")
        root_asked = sem("root_asked")
        root_ready = sem("root_ready")
        rows_ready = sem("rows_ready")
        rows_turned = sem("rows_turned")
        hT_high_ready = sem("hT_high_ready")
        hT_ready = sem("hT_ready")
        rows_cleared = sem("rows_cleared")
        logits_ready = sem("logits_ready")
        e_shifted = sem("e_shifted")
        e_exp_ready = sem("e_exp_ready")
        chosen_ready = sem("chosen_ready")
        ranks_ready = sem("ranks_ready")
        experts_ready = sem("experts_ready")
        slots_ready = sem("slots_ready")
        scattered = sem("scattered")
        weights_loaded = [sem("weights_even_loaded"), sem("weights_odd_loaded")]
        block_loaded = [sem("block_even_loaded"), sem("block_odd_loaded")]
        block_turned = sem("block_turned")
        block_high_ready = sem("block_high_ready")
        block_T_ready = sem("block_T_ready")
        w13_high_ready = sem("w13_high_ready")
        w13_ready = sem("w13_ready")
        w2_high_ready = sem("w2_high_ready")
        w2_ready = sem("w2_ready")
        product_ready = sem("product_ready")
        gated_high_ready = sem("gated_high_ready")
        up_ready = sem("up_ready")
        relu_ready = sem("relu_ready")
        gated_ready = sem("gated_ready")
        down_done = sem("down_done")
        result_ready = sem("result_ready")
        result_stored = [sem("result_even_stored"), sem("result_odd_stored")]
        gathered = [sem(f"gathered{b}") for b in range(B)]
        stored = sem("stored")
        out_ready = sem("out_ready")
        shift_ready = sem("shift_ready")
        acc_normed = sem("acc_normed")

        def attention_sems(tag):
            names = ["w_loaded", "w_high_ready", "w_ready", "wo_loaded", "wo_high_ready", "wo_ready",
                     "oT_high_ready", "proj_psum_ready", "x_bank_empty", "cos_ready", "sin_ready",
                     "first_high_ready",
                     "high_ready", "q_ready", "k_ready", "v_psum_ready", "scores_ready", "max_ready", "probs_ready",
                     "rinv_ready", "norm_ready", "pt_psum_ready", "pt_ready", "o_psum_ready", "o_bank_empty",
                     "y_psum_ready"]
            return {n: sem(f"{n}_{tag}") for n in names}

        class Phase:
            def __init__(self, number, head, w_dram, o_dram, slots):
                self.number = number
                self.first = number == 0
                self.sems = attention_sems("ab"[number])
                self.units = QROWS // head * QT
                self.group = self.units // QTILES
                self.w_dram, self.o_dram = w_dram, o_dram
                self.slots = {u: list(ev) for u, ev in slots.items()}
                for j in range(QTILES):
                    u = (j + 1) * self.group - 1 + LAG + VALUES_LAG
                    self.slots.setdefault(u % self.units, []).append(("values", j, -(u // self.units)))

            def events(self, u, kind):
                return [e for e in self.slots.get(u, []) if kinds[kind](e)]

            def values_before(self, u, back):
                slot, d = (u - back, 0) if u >= back else (self.units + u - back, -1)
                return [(e[1], e[2] + d) for e in self.slots.get(slot, []) if e[0] == "values"]

            def before(self, of, event, kind):
                n = 0
                for u in range(self.units):
                    for e in self.slots.get(u, []):
                        if e == event:
                            return n
                        n += kinds[kind](e) and e[2] in of
                raise ValueError(event)

            def per_step(self, of, kind):
                return sum(kinds[kind](e) and e[2] in of for ev in self.slots.values() for e in ev)

            def number_of(self, s, event, kind):
                start = PROLOGUE[kind]
                if isinstance(s, int) and s == 0:
                    return start + self.before((0, 1), event, kind)
                if isinstance(s, int) and s == STEPS - 1:
                    of = (-1, 0)
                elif isinstance(s, int) and s == STEPS:
                    of = (-1,)
                else:
                    of = (-1, 0, 1)
                full = self.per_step((-1, 0, 1), kind)
                start += self.per_step((0, 1), kind)
                if isinstance(s, int) and s == STEPS:
                    return (start + full * (STEPS - 2) + self.per_step((-1, 0), kind)
                            + self.before(of, event, kind))
                return full * (s - 1) + start + self.before(of, event, kind)

            def parity_of(self, s, parity, event):
                return self.number_of(s if isinstance(s, int) else 2 - parity, event, "rotate") % 2

            def two_before(self, s, event):
                row = [e for u in sorted(self.slots) for e in self.events(u, "rotate")]
                n = row.index(event)
                _, t, d = row[n - 2]
                d -= n < 2
                return ("k_ready", s + d + 1) if t == T_K else ("q_ready", QTILES * (s + d) + t + 1)

        kinds = {
            "x": lambda e: e[0] in ("project", "output"),
            "o": lambda e: e[0] in ("values", "turn_v"),
            "project": lambda e: e[0] == "project",
            "rotate": lambda e: e[0] == "project" and e[1] != T_V,
        }
        FIRST_TILES = (T_K, 0, 1, 2)
        PROLOGUE = {"x": 4, "o": 0, "project": 4, "rotate": 4}
        SPLIT_BY_VECTOR = 2

        phases = [
            Phase(0, D1, wa_in, oa_in, {
                0: [("project", 3, 0)], 1: [("split_o", 0, -1)], 2: [("project", T_V, 0)],
                3: [("split_o", 1, -1)], 4: [("split_o", 2, -1)], 5: [("project", T_K, 1)],
                6: [("turn_v", 0, 0), ("split_o", 3, -1)], 7: [("project", 0, 1)], 9: [("project", 1, 1)],
                10: [("output", 0, -1)], 12: [("output", 1, -1)], 14: [("project", 2, 1)]}),
            Phase(1, D2, wb_in, ob_in, {
                0: [("project", 3, 0)], 2: [("project", T_V, 0)], 3: [("split_o", 0, -1)],
                5: [("turn_v", 0, 0), ("split_o", 1, -1)], 6: [("split_o", 2, -1)], 7: [("split_o", 3, -1)],
                9: [("project", T_K, 1)], 11: [("output", 0, -1)], 14: [("output", 1, -1)],
                17: [("project", 0, 1)], 21: [("project", 1, 1)], 26: [("project", 2, 1)]}),
        ]
        PROBS0, PTPSUM0, PT0, OPSUM0 = N_SCORE, N_PROB, N_TURN, 2
        PRODUCT0, DOWN0, RESULT0 = N_UP, FT, 2

        def steps(eng, slot, ph):
            def step(s, parity, of, upto=ph.units):
                for u in range(upto):
                    slot(s, parity, u, of)
            step(0, 0, (0, 1))
            with eng.Fori(0, (STEPS - 2) // 2) as pair:
                step(2 * pair + 1, 1, (-1, 0, 1))
                step(2 * pair + 2, 0, (-1, 0, 1))
            step(STEPS - 1, 1, (-1, 0))
            step(STEPS, 0, (-1,), max(u for u, ev in ph.slots.items() if any(e[2] == -1 for e in ev)) + 1)

        def unit_at(ph, s, u, back, of):
            if u >= back:
                return (s, u - back) if 0 in of else None
            return (s - 1, ph.units + u - back) if -1 in of else None

        block = ctx.enter_context(nc.Block())

        @block.sync
        def _(sp):
            x_v = x_in.rearrange("(i p) h -> p i h", p=P)
            sp.dma_start(x[:, :, :], x_v).then_inc(x_loaded, 16)
            sp.dma_start(ln_w[:, :, :], ln_in).then_inc(tables_loaded, 16)
            sp.dma_start(bias[:, :, :], ba_in).then_inc(tables_loaded, 16)
            sp.dma_start(cosT[:, :], cos_in).then_inc(tables_loaded, 16)
            sp.dma_start(sinT[:, :], sin_in).then_inc(tables_loaded, 16)
            sp.dma_start(gate_w[:, :, :], gate_in.rearrange("(k p) e -> p k e", p=P)).then_inc(tables_loaded, 16)

            def load_w(ph, s):
                sp.dma_start(w_qkv[:, :, :], ph.w_dram[bass.ds((s % G) * H, H), :]
                             .rearrange("(k p) n -> p k n", p=P)).then_inc(ph.sems["w_loaded"], 16)

            def load_wo(ph, s):
                sp.dma_start(w_o[:, :, :], ph.o_dram[bass.ds((s % G) * QROWS, QROWS), :]
                             .rearrange("(k p) n -> p k n", p=P)).then_inc(ph.sems["wo_loaded"], 16)

            def load_expert(j, par):
                e = sp.value_load(block_expert[0:1, bass.ds(j, 1)], min_val=0, max_val=E - 1)
                for dst, src, rows in ((w13[par][:, 0, :, :], w1_in, H), (w13[par][:, 1, :, :], w3_in, H),
                                       (w2[par][:, :, :], w2_in, F)):
                    sp.dma_start(dst, src[bass.ds(e * rows, rows), :].rearrange("(k p) n -> p k n", p=P))\
                        .then_inc(weights_loaded[par], 16)

            def load_block(j, par):
                sp.dma_start(slot_tok[:, par, :, :], slot_rows[bass.ds(j * SLOTS, SLOTS), :]
                             .rearrange("(a p) h -> p a h", p=P)).then_inc(block_loaded[par], 16)

            def store_result(j, par):
                sp.wait_ge(result_ready, RESULT0 + j + 1)
                sp.dma_start(slot_results[bass.ds(j * SLOTS, SLOTS), :].rearrange("(a p) h -> p a h", p=P),
                             result[:, par, :, :]).then_inc(result_stored[par], 16)

            load_w(phases[0], 0)
            load_wo(phases[0], 0)
            rows = slot_rows.rearrange("(p r) h -> p (r h)", p=P)
            width = rows.shape[1]
            sp.wait_ge(acc_cleared, 3)
            pieces = list(range(0, width, TILES * H))
            for at in pieces:
                n = min(TILES * H, width - at)
                sp.dma_start(rows[:, at:at + n], acc[:, :, :].rearrange("p i h -> p (i h)")[:, 0:n])\
                    .then_inc(rows_cleared, 16)

            for ph in phases:
                c = ph.sems
                if not ph.first:
                    load_w(ph, 0)
                    load_wo(ph, 0)

                for s in (1, 2):
                    sp.wait_ge(c["w_ready"], PROJ * s)
                    load_w(ph, s)
                with sp.Fori(2, STEPS) as s:
                    sp.wait_ge(c["w_ready"], PROJ * (s + 1))
                    load_w(ph, s + 1)
                    sp.wait_ge(c["wo_ready"], QTILES * (s - 1))
                    load_wo(ph, s - 1)
                sp.wait_ge(c["wo_ready"], QTILES * (STEPS - 1))
                load_wo(ph, STEPS - 1)
                sp.wait_ge(c["x_bank_empty"], ph.number_of(STEPS, ("output", 1, -1), "x") + 1)
            sp.wait_ge(experts_ready, 1)
            load_expert(0, 0)
            load_expert(1, 1)
            sp.wait_ge(scattered, 16 * TOPK * TILES)
            load_block(0, 0)
            load_block(1, 1)

            def next_block(j, par):
                sp.wait_ge(w13_ready, FT * (j - 1))
                sp.wait_ge(w2_ready, FT * (j - 1))
                load_expert(j, par)
                sp.wait_ge(block_turned, j - 1)
                load_block(j, par)
                store_result(j - 2, par)
            with sp.Fori(1, BLOCKS // 2) as pair:
                for par in range(2):
                    next_block(2 * pair + par, par)
            next_block(BLOCKS - 1, 0)
            store_result(BLOCKS - 2, 1)
            store_result(BLOCKS - 1, 0)
            out_v = out.rearrange("(i p) h -> p i h", p=P)
            for b in range(B):
                sp.wait_ge(out_ready, b + 1)
                at = slice(b * QT, (b + 1) * QT)
                sp.dma_start(out_v[:, at, :], x[:, at, :]).then_inc(stored, 16)
            sp.wait_ge(stored, 16 * B)

        @block.gpsimd
        def _(pool):
            pool.memset(identity[:, :], 0.0).then_inc(acc_cleared, 1)
            pool.memset(causal[:, :], 0.0).then_inc(acc_cleared, 1)
            pool.wait_ge(acc_cleared, 2)
            pool.affine_select(out=identity[:, :], in_=identity[:, :], compare_op=ALU.not_equal, fill=1.0,
                               base=0, pattern=[[-1, P]], channel_multiplier=1).then_inc(consts_ready, 1)
            pool.affine_select(out=causal[:, :], in_=causal[:, :], compare_op=ALU.is_ge, fill=MASKED,
                               base=0, pattern=[[-1, P]], channel_multiplier=1).then_inc(consts_ready, 1)
            pool.iota(iota_i[:, :, :], pattern=[[0, TILES], [1, E]], base=0, channel_multiplier=0)\
                .then_inc(consts_ready, 1)
            pool.iota(block_start_i[:, :, :], pattern=[[SLOTS, BLOCKS], [0, E]], base=0, channel_multiplier=0)\
                .then_inc(consts_ready, 1)
            pool.memset(acc[:, :, :], 0.0).then_inc(acc_cleared, 1)
            pool.memset(ones[:, :], 1.0).then_inc(acc_cleared, 1)
            pool.wait_ge(consts_ready, 4)
            pool.tensor_copy(identity_b[:, :], identity[:, :]).then_inc(small_ready, 1)
            pool.tensor_copy(causal_b[:, :], causal[:, :]).then_inc(small_ready, 1)
            pool.tensor_copy(iota_e[:, :, :], iota_i[:, :, :]).then_inc(small_ready, 1)
            pool.tensor_copy(block_start[:, :, :], block_start_i[:, :, :]).then_inc(small_ready, 1)
            pool.memset(ones_b[:, :], 1.0).then_inc(small_ready, 1)
            pool.wait_ge(small_ready, 5)
            pool.affine_select(out=earlier_b[:, :], in_=ones_b[:, :], compare_op=ALU.is_gt, fill=0.0,
                               base=0, pattern=[[1, P]], channel_multiplier=-1).then_inc(small_ready, 1)

            pool.wait_ge(acc_cleared, 4)
            pool.wait_ge(tables_loaded, 5 * 16)

            def attention(ph):
                c = ph.sems

                def take_projected(sp_, t, parity, i, x_number, number):
                    pool.wait_ge(c["x_bank_empty"], x_number + 1)
                    if ph.first:
                        pool.tensor_tensor(times_cos[:, i, :], projected[:, i, :], cosT[:, :], ALU.mult)\
                            .then_inc(c["cos_ready"], 1)
                        return
                    high_seen = number + 1 - SPLIT_BY_VECTOR
                    if isinstance(sp_, int) and number == SPLIT_BY_VECTOR:
                        pool.wait_ge(c["q_ready"], 1)
                    if t < T_K:
                        if not (isinstance(sp_, int) and sp_ == 0):
                            pool.wait_ge(c["scores_ready"], (sp_ - 1) * ph.units + (t + 1) * ph.group)
                        halves = (slice(0, D2), slice(D2, P))
                        for n in range(2):
                            part = projected[halves[n], i, :]
                            ins = pool.tensor_tensor(q_hl[halves[n], 2 * t + n, :], part,
                                                     ones[halves[n], 0:1].broadcast_to([D2, S]), ALU.mult)
                        ins.then_inc(c["high_ready"], 1)
                        pool.wait_ge(c["high_ready"], high_seen)
                        for n in range(2):
                            ins = pool.tensor_tensor(q_hl[halves[1 - n], 2 * t + n, :], projected[halves[n], i, :],
                                                     q_hl[halves[n], 2 * t + n, :].bitcast(F32), ALU.subtract)
                        ins.then_inc(c["q_ready"], 1)
                        pool.wait_ge(c["q_ready"], QTILES * sp_ + t + 1)
                        return
                    buf = parity
                    for kv in range(2):
                        rows = slice(kv * D2, (kv + 1) * D2)
                        for half in range(2):
                            part = projected[rows, i, :]
                            ins = pool.tensor_tensor(k_hi[half * D2:(half + 1) * D2, buf, kv, :], part,
                                                     ones[rows, 0:1].broadcast_to([D2, S]), ALU.mult)
                    ins.then_inc(c["high_ready"], 1)
                    pool.wait_ge(c["high_ready"], high_seen)
                    for kv in range(2):
                        rows = slice(kv * D2, (kv + 1) * D2)
                        for half in range(2):
                            ins = pool.tensor_tensor(k_lo[half * D2:(half + 1) * D2, buf, kv, :],
                                                     projected[rows, i, :], k_hi[rows, buf, kv, :].bitcast(F32),
                                                     ALU.subtract)
                    ins.then_inc(c["k_ready"], 1)
                    pool.wait_ge(c["k_ready"], sp_ + 1)

                def split_w(t, number):
                    cols = slice(t * P, (t + 1) * P)
                    pool.wait_ge(c["w_high_ready"], number + 1)
                    pool.tensor_tensor(w_lo[:, :, cols], w_qkv[:, :, cols], w_hi[:, :, cols].bitcast(F32),
                                       ALU.subtract).then_inc(c["w_ready"], 1)
                    pool.wait_ge(c["w_ready"], number + 1)

                def split_wo(s, j):
                    pool.wait_ge(c["wo_high_ready"], s + 1)
                    pool.tensor_tensor(wo_lo[:, j, :], w_o[:, j, :], wo_hi[:, j, :].bitcast(F32), ALU.subtract)\
                        .then_inc(c["wo_ready"], 1)
                    pool.wait_ge(c["wo_ready"], QTILES * s + j + 1)

                for n, t in enumerate(FIRST_TILES + (3, T_V)):
                    split_w(t, n)
                for n, t in enumerate(FIRST_TILES):
                    if ph.first or n >= SPLIT_BY_VECTOR:
                        take_projected(0, t, 0, n % 2, n, n)
                for n, t in enumerate(FIRST_TILES):
                    split_w(t, PROJ + n)

                def slot(s, parity, u, of):
                    for e in ph.slots.get(u, []):
                        kind, arg, d = e
                        if d not in of:
                            continue
                        if kinds["rotate"](e):
                            take_projected(s + d, arg, (parity + d) % 2, ph.parity_of(s, parity, e),
                                           ph.number_of(s, e, "x"), ph.number_of(s, e, "rotate"))
                        elif kind == "split_o":
                            split_wo(s + d, arg)
                    for e in ph.slots.get(u - 1, []):
                        kind, arg, d = e
                        if kind == "project" and d in of and 1 in of:
                            split_w(arg, ph.number_of(s, e, "project") + PROJ)
                steps(pool, slot, ph)
            attention(phases[0])
            attention(phases[1])

            pool.wait_ge(rows_cleared, 16 * len(range(0, BLOCKS * SLOTS // P * H, TILES * H)))
            for n in range(TOPK):
                pool.wait_ge(slots_ready, n + 1)
                for i in range(TILES):
                    pool.indirect_dma_start(out=slot_rows, out_offset=bass.IndirectOffsetOnAxis(
                        ap=slot_of[n][:, i:i + 1], axis=0), in_=htok[:, i, :], in_offset=None)\
                        .then_inc(scattered, 16)

            def split_w2(j, par):
                for f in range(FT):
                    pool.wait_ge(down_done, FT * j + f + 1)
                    pool.tensor_tensor(w2_hi[:, f, :], w2[par][:, f, :], ones[:, 0:1].broadcast_to([P, H]), ALU.mult)\
                        .then_inc(w2_high_ready, 1)
                    pool.wait_ge(w2_high_ready, FT * j + f + 1)
                    pool.tensor_tensor(w2_lo[:, f, :], w2[par][:, f, :], w2_hi[:, f, :].bitcast(F32), ALU.subtract)\
                        .then_inc(w2_ready, 1)

            for j in range(2):
                pool.wait_ge(weights_loaded[j], 48)
                split_w2(j, j)
            with pool.Fori(1, BLOCKS // 2) as pair:
                for par in range(2):
                    pool.wait_ge(weights_loaded[par], 48 * (pair + 1))
                    split_w2(2 * pair + par, par)
            pool.wait_ge(weights_loaded[0], 48 * (BLOCKS // 2 + 1))
            split_w2(BLOCKS - 1, 0)

            for par in range(2):
                pool.wait_ge(result_stored[par], 16 * (1 + (BLOCKS + 1 - par) // 2))
            for i in range(TILES):
                for n, dst in enumerate((htok[:, :, :], hT_rows)):
                    pool.indirect_dma_start(out=dst[:, i, :], out_offset=None, in_=slot_results,
                                            in_offset=bass.IndirectOffsetOnAxis(ap=slot_of[n][:, i:i + 1], axis=0))\
                        .then_inc(gathered[i // QT], 16)

        @block.tensor
        def _(pe):
            def turn_rows(norm):
                for b in range(B):
                    pe.wait_ge(rows_ready, B * norm + b + 1)
                    for k in range(KT):
                        for i in range(QT):
                            mm = pe.transpose(bank[KT * b + k][:, i * P:(i + 1) * P],
                                              htok[:, QT * b + i, k * P:(k + 1) * P], identity[:, :])
                        mm.then_inc(rows_turned, 1)
                pe.wait_ge(hT_ready, B * KT * (norm + 1))

            def attention(ph):
                c = ph.sems

                def project(sp_, t, x_number, number):
                    if x_number is not None:
                        pe.wait_ge(c["x_bank_empty"], x_number)
                    pe.wait_ge(c["w_ready"], number + 1)
                    rows, cols = bass.ds(sp_ // G * S, S), slice(t * P, (t + 1) * P)
                    for k in range(KT):
                        pe.matmul(x_bank[:, :], w_hi[:, k, cols], hT_hi[:, k, rows], start=(k == 0), stop=False)
                        pe.matmul(x_bank[:, :], w_hi[:, k, cols], hT_lo[:, k, rows], start=False, stop=False)
                        mm = pe.matmul(x_bank[:, :], w_lo[:, k, cols], hT_hi[:, k, rows],
                                       start=False, stop=(k == KT - 1))
                    mm.then_inc(c["proj_psum_ready"], 1)

                def turn_v(x_number, o_number):
                    pe.wait_ge(c["x_bank_empty"], x_number + 1)
                    if not (isinstance(o_number, int) and o_number == 0):
                        pe.wait_ge(c["o_bank_empty"], o_number)
                    for i in range(QT):
                        mm = pe.transpose(o_bank[:, i * P:(i + 1) * P], vT[:, i * P:(i + 1) * P], identity[:, :])
                    mm.then_inc(c["v_psum_ready"], 1)

                def scores(s, parity, u):
                    h, q = u // QT, Q_ORDER[u % QT]
                    w = (q + 1) * P
                    dst = score_bank[u % N_SCORE]
                    if u % ph.group == 0:
                        pe.wait_ge(c["q_ready"], QTILES * s + u // ph.group + 1)
                    if u == 0:
                        pe.wait_ge(c["k_ready"], s + 1)
                    pe.wait_ge(c["probs_ready"], s * ph.units + u + 1)
                    if ph.first:
                        pe.matmul(dst[:, 0:w], qT[:, h, q * P:w], kT[:, parity, 0:w], start=True, stop=False)
                    else:
                        kv, wide = h // 4, max(w, 2 * P)
                        for n, part in enumerate((k_hi, k_lo)):
                            pe.matmul(dst[:, 0:wide], q_hl[:, h, q * P:w], part[:, parity, kv, 0:wide],
                                      start=(n == 0), stop=False)
                    pe.matmul(dst[:, q * P:w], identity_b[:, :], causal_b[:, :], start=False, stop=True)\
                        .then_inc(c["scores_ready"], 1)

                def turn(s, u):
                    q = Q_ORDER[u % QT]
                    pe.wait_ge(c["norm_ready"], s * ph.units + u + 1)
                    pe.wait_ge(c["pt_ready"], s * ph.units + u + 1)
                    for k in range(q + 1):
                        mm = pe.transpose(turn_bank[u % N_TURN][:, k * P:(k + 1) * P],
                                          probs[:, u % N_PROB, k * P:(k + 1) * P], identity[:, :])
                    mm.then_inc(c["pt_psum_ready"], 1)

                def values(s, parity, j, o_number):
                    pe.wait_ge(c["o_bank_empty"], o_number)
                    pe.wait_ge(c["pt_ready"], PT0 + s * ph.units + (j + 1) * ph.group)
                    for k in range(QT):
                        if ph.first:
                            mm = pe.matmul(o_bank[:, k * P:S], v[:, parity, k, :], probsT[:, j % 2, 0, k, k * P:S],
                                           start=(k == 0), stop=(k == QT - 1))
                        else:
                            kv = j // 2
                            for i in range(2):
                                mm = pe.matmul(o_bank[i * D2:(i + 1) * D2, k * P:S],
                                               v[:, parity, k, kv * D2:(kv + 1) * D2],
                                               probsT[:, j % 2, i, k, k * P:S], start=(k == 0), stop=(k == QT - 1))
                    mm.then_inc(c["o_psum_ready"], 1)

                def output(s, i, x_number, o_number):
                    if i == 0:
                        pe.wait_ge(c["wo_ready"], QTILES * (s + 1))
                        pe.wait_ge(c["o_bank_empty"], o_number + 1)
                    pe.wait_ge(c["x_bank_empty"], x_number)
                    for q in range(2 * i, 2 * i + 2):
                        half, rows = x_bank[:, (q % 2) * H:(q % 2 + 1) * H], slice(q * P, (q + 1) * P)
                        for j in range(QTILES):
                            pe.matmul(half, oT_hi[:, j, rows], wo_hi[:, j, :], start=(j == 0), stop=False)
                            pe.matmul(half, oT_hi[:, j, rows], wo_lo[:, j, :], start=False, stop=False)
                            mm = pe.matmul(half, oT_lo[:, j, rows], wo_hi[:, j, :],
                                           start=False, stop=(j == QTILES - 1))
                    mm.then_inc(c["y_psum_ready"], 1)

                pe.sem_inc(c["pt_psum_ready"], PTPSUM0)
                pe.sem_inc(c["o_psum_ready"], OPSUM0)
                for n, t in enumerate(FIRST_TILES):
                    project(0, t, n or None, n)

                def slot(s, parity, u, of):
                    if 0 in of and u < ph.units:
                        scores(s, parity, u)
                    back = unit_at(ph, s, u, LAG, of)
                    if back:
                        turn(*back)
                    for e in ph.slots.get(u, []):
                        kind, arg, d = e
                        if d not in of:
                            continue
                        if kind == "project":
                            project(s + d, arg, ph.number_of(s, e, "x"), ph.number_of(s, e, "project"))
                        elif kind == "turn_v":
                            turn_v(ph.number_of(s, ("project", T_V, 0), "x"), ph.number_of(s, e, "o"))
                        elif kind == "values":
                            values(s + d, (parity + d) % 2, arg, ph.number_of(s, e, "o"))
                        elif kind == "output":
                            output(s + d, arg, ph.number_of(s, e, "x"),
                                   ph.number_of(s, ("values", QTILES - 1, -1), "o"))
                steps(pe, slot, ph)

            pe.wait_ge(consts_ready, 2)
            pe.wait_ge(small_ready, 2)
            for ph in phases:
                turn_rows(ph.number)
                attention(ph)

            turn_rows(2)
            for i in range(TILES):
                for k in range(KT):
                    mm = pe.matmul(router_bank[:, i * E:(i + 1) * E], hT[:, k, i * P:(i + 1) * P], gate_w[:, k, :],
                                   start=(k == 0), stop=(k == KT - 1))
            mm.then_inc(logits_ready, 1)
            pe.wait_ge(small_ready, 6)
            pe.wait_ge(chosen_ready, 1)
            pe.matmul(router_bank[:, 0:TILES * E], earlier_b[:, :], chosen_b[:, :], start=True, stop=True)
            pe.matmul(router_bank[:, TILES * E:2 * TILES * E], ones_b[:, :], chosen_b[:, :], start=True, stop=True)\
                .then_inc(ranks_ready, 1)

            pe.sem_inc(down_done, DOWN0)

            def turn_block(j, par):
                pe.wait_ge(block_loaded[par], 16 * (j // 2 + 1))
                if not (isinstance(j, int) and j == 0):
                    pe.wait_ge(block_T_ready, j)
                for k in range(KT):
                    for a in range(SA):
                        mm = pe.transpose(slot_bank[:, k * SLOTS + a * P:k * SLOTS + (a + 1) * P],
                                          slot_tok[:, par, a, k * P:(k + 1) * P], identity[:, :])
                mm.then_inc(block_turned, 1)

            def expert_block(j, par, last=False):
                def up(f):
                    dst = up_bank[f % N_UP]
                    cols = slice(f * P, (f + 1) * P)
                    pe.wait_ge(product_ready, FT * j + f + 1)
                    pe.wait_ge(w13_ready, FT * j + f + 1)
                    for n in range(2):
                        half = dst[:, n * SLOTS:(n + 1) * SLOTS]
                        for k in range(KT):
                            pe.matmul(half, w13_hi[:, n, k, cols], slot_hi[:, par, k, :], start=(k == 0), stop=False)
                            pe.matmul(half, w13_hi[:, n, k, cols], slot_lo[:, par, k, :], start=False, stop=False)
                            mm = pe.matmul(half, w13_lo[:, n, k, cols], slot_hi[:, par, k, :],
                                           start=False, stop=(k == KT - 1))
                    mm.then_inc(up_ready, 1)

                def down(f):
                    if f == 0:
                        pe.wait_ge(result_ready, j + 1)
                    pe.wait_ge(w2_ready, FT * j + f + 1)
                    pe.wait_ge(gated_ready, FT * j + f + 1)
                    i = f % N_GATED
                    for a in range(SA):
                        half, rows = down_bank[par][:, a * H:(a + 1) * H], slice(a * P, (a + 1) * P)
                        pe.matmul(half, gated_hi[:, i, rows], w2_hi[:, f, :], start=(f == 0 and a == 0), stop=False,
                                  skip_group_check=True)
                        pe.matmul(half, gated_hi[:, i, rows], w2_lo[:, f, :], start=False, stop=False,
                                  skip_group_check=True)
                        mm = pe.matmul(half, gated_lo[:, i, rows], w2_hi[:, f, :], start=False, stop=(f == FT - 1),
                                       skip_group_check=True)
                    mm.then_inc(down_done, 1)

                pe.wait_ge(block_T_ready, j + 1)
                for f in range(FT + DOWN_LAG):
                    if f < FT:
                        up(f)
                    if f == FT - 1 and not last:
                        turn_block(j + 1, 1 - par)
                    if f >= DOWN_LAG:
                        down(f - DOWN_LAG)

            turn_block(0, 0)
            with pe.Fori(0, BLOCKS // 2) as pair:
                for par in range(2):
                    expert_block(2 * pair + par, par)
            expert_block(BLOCKS - 1, 0, True)

        @block.scalar
        def _(act):
            roots = [0]

            def root_of_square(at=slice(0, TILES)):
                roots[0] += 1
                act.wait_ge(root_asked, roots[0])
                act.activation(root[:, at], square[:, at], ACT.Sqrt).then_inc(root_ready, 1)

            def norm_acc(tiles):
                act.wait_ge(shift_ready, 1)
                for i in tiles:
                    ins = act.activation(acc[:, i, :], acc[:, i, :], ACT.Identity, scale=inv1[:, i:i + 1],
                                         bias=shift[:, i:i + 1])
                ins.then_inc(acc_normed, 1)

            def take_rows(norm):
                if norm == 0:
                    act.wait_ge(tables_loaded, 5 * 16)
                dst, done = (hT, hT_ready) if norm == 2 else (hT_hi, hT_high_ready)
                for b in range(B):
                    for k in range(KT):
                        act.wait_ge(rows_turned, B * KT * norm + KT * b + k + 1)
                        act.activation(dst[:, k, b * S:(b + 1) * S], bank[KT * b + k][:, :], ACT.Copy,
                                       scale=ln_w[:, norm, k:k + 1]).then_inc(done, 1)

            def attention(ph):
                c = ph.sems
                act.sem_inc(c["probs_ready"], PROBS0)
                act.sem_inc(c["pt_ready"], PT0)

                def split_w(t, number, step):
                    if t == T_K:
                        act.wait_ge(c["w_loaded"], 16 * (step + 1))
                    if not (isinstance(number, int) and number < PROJ):
                        act.wait_ge(c["proj_psum_ready"], number + 1 - PROJ)
                    cols = slice(t * P, (t + 1) * P)
                    act.activation(w_hi[:, :, cols], w_qkv[:, :, cols], ACT.Copy).then_inc(c["w_high_ready"], 1)

                def split_wo(s):
                    act.wait_ge(c["wo_loaded"], 16 * (s + 1))
                    if not (isinstance(s, int) and s == 0):
                        act.wait_ge(c["y_psum_ready"], 2 * s)
                    act.activation(wo_hi[:, :, :], w_o[:, :, :], ACT.Copy).then_inc(c["wo_high_ready"], 1)

                def take_values(s, j):
                    act.wait_ge(c["o_psum_ready"], OPSUM0 + QTILES * s + j + 1)
                    if j == 0 and not (isinstance(s, int) and s == 0):
                        act.wait_ge(c["y_psum_ready"], 2 * s)
                    act.activation(oT_hi[:, j, :], o_bank[:, :], ACT.Copy).then_inc(c["oT_high_ready"], 1)

                def take_projection(sp_, t, i, number, before):
                    act.wait_ge(c["proj_psum_ready"], number + 1)
                    if t == T_V:
                        dst = vT[:, :]
                        before = ("v_psum_ready", sp_)
                    else:
                        dst = projected[:, i, :]
                    if before[0] and not (isinstance(before[1], int) and before[1] == 0):
                        act.wait_ge(c[before[0]], before[1])
                    if ph.first:
                        ins = act.activation(dst, x_bank[:, :], ACT.Identity, bias=bias[:, bass.ds(sp_ % G, 1), t])
                    elif t < T_K:
                        ins = act.activation(dst, x_bank[:, :], ACT.Copy, scale=D2 ** -0.5)
                    else:
                        ins = act.activation(dst, x_bank[:, :], ACT.Copy)
                    ins.then_inc(c["x_bank_empty"], 1)

                def take_v(sp_, parity):
                    act.wait_ge(c["v_psum_ready"], sp_ + 1)
                    act.activation(v[:, parity, :, :], o_bank[:, :].rearrange("p (i d) -> p i d", i=QT), ACT.Copy)\
                        .then_inc(c["o_bank_empty"], 1)

                def exponentials(s, u):
                    w = (Q_ORDER[u % QT] + 1) * P
                    i = u % N_PROB
                    act.wait_ge(c["max_ready"], s * ph.units + u + 1)
                    act.wait_ge(c["pt_psum_ready"], s * ph.units + u + 1)
                    act.activation(probs[:, i, 0:w], score_bank[u % N_SCORE][:, 0:w], ACT.Exp,
                                   bias=negmax[:, i:i + 1], accum_out=rowsum[:, i:i + 1])\
                        .then_inc(c["probs_ready"], 1)

                def take_turned(s, u):
                    q = Q_ORDER[u % QT]
                    j = u // ph.group
                    i = 0 if ph.first else u // QT % 2
                    act.wait_ge(c["pt_psum_ready"], PTPSUM0 + s * ph.units + u + 1)
                    if u % ph.group == 0:
                        act.wait_ge(c["o_psum_ready"], QTILES * s + j + 1)
                    act.activation(probsT[:, j % 2, i, 0:q + 1, q * P:(q + 1) * P],
                                   turn_bank[u % N_TURN][:, 0:(q + 1) * P].rearrange("p (k n) -> p k n", n=P),
                                   ACT.Copy).then_inc(c["pt_ready"], 1)

                for n, t in enumerate(FIRST_TILES + (3, T_V)):
                    split_w(t, n, 0)
                if not ph.first:
                    root_of_square()
                    norm_acc(range(TILES // 2, TILES))
                root_of_square()
                root_of_square()
                take_rows(ph.number)
                for n, t in enumerate(FIRST_TILES):
                    before = ("k_ready", 1) if n == 2 else ("q_ready", max(n - 2, 0))
                    take_projection(0, t, n % 2, n, before)
                for n, t in enumerate(FIRST_TILES):
                    split_w(t, PROJ + n, 1)

                def slot(s, parity, u, of):
                    back = unit_at(ph, s, u, LAG, of)
                    if back:
                        take_turned(*back)
                    if 0 in of and u < ph.units:
                        exponentials(s, u)
                    for j, d in ph.values_before(u, 1):
                        if d in of:
                            take_values(s + d, j)
                    for e in ph.slots.get(u, []):
                        kind, arg, d = e
                        if d not in of:
                            continue
                        if kind == "project" and arg == T_V:
                            take_projection(s + d, arg, None, ph.number_of(s, e, "project"), None)
                        elif kind == "project":
                            take_projection(s + d, arg, ph.parity_of(s, parity, e), ph.number_of(s, e, "project"),
                                            ph.two_before(s, e))
                        elif kind == "turn_v":
                            take_v(s + d, (parity + d) % 2)
                        elif kind == "split_o" and arg == 0:
                            split_wo(s + d)
                    for e in ph.slots.get(u - 1, []):
                        kind, arg, d = e
                        if kind == "project" and d in of and 1 in of:
                            split_w(arg, ph.number_of(s, e, "project") + PROJ, s + d + 1)
                steps(act, slot, ph)

            for ph in phases:
                attention(ph)
            root_of_square()
            take_rows(2)
            act.wait_ge(e_shifted, 1)
            act.activation(e_prob[:, :, :], pick[:, :, :], ACT.Exp).then_inc(e_exp_ready, 1)

            def take_block(j, par):
                act.wait_ge(block_turned, j + 1)
                for k in range(KT):
                    ins = act.activation(slot_hi[:, par, k, :], slot_bank[:, k * SLOTS:(k + 1) * SLOTS], ACT.Copy,
                                         scale=ln_w[:, 2, k:k + 1])
                ins.then_inc(block_high_ready, 1)

            def split_high(j, par, f):
                cols = slice(f * P, (f + 1) * P)
                if f == 0:
                    act.wait_ge(weights_loaded[par], 48 * (j // 2 + 1))
                act.wait_ge(down_done, FT * j + f + 1)
                act.activation(w13_hi[:, :, :, cols].rearrange("p n k c -> p (n k) c"),
                               w13[par][:, :, :, cols].rearrange("p n k c -> p (n k) c"), ACT.Copy)\
                    .then_inc(w13_high_ready, 1)

            def expert_block(j, par, last=False):
                for f in range(FT + SPLIT_LAG):
                    if f < FT:
                        act.wait_ge(up_ready, FT * j + f + 1)
                        act.activation(rectified[:, f % N_UP, :], up_bank[f % N_UP][:, 0:SLOTS], ACT.Relu)\
                            .then_inc(relu_ready, 1)
                    if 1 <= f <= FT:
                        g = f - 1
                        act.wait_ge(product_ready, PRODUCT0 + FT * j + g + 1)
                        act.activation(gated_hi[:, g % N_GATED, :], gated[:, g % N_GATED, :], ACT.Copy)\
                            .then_inc(gated_high_ready, 1)
                    if f == FT and not last:
                        take_block(j + 1, 1 - par)
                    if f >= SPLIT_LAG and not last:
                        split_high(j + 1, 1 - par, f - SPLIT_LAG)

            for f in range(FT):
                split_high(0, 0, f)
            take_block(0, 0)
            with act.Fori(0, BLOCKS // 2) as pair:
                for par in range(2):
                    expert_block(2 * pair + par, par)
            expert_block(BLOCKS - 1, 0, True)
            for b in range(B):
                root_of_square(slice(b * QT, (b + 1) * QT))

        @block.vector
        def _(dve):
            count = [0, 0]

            def link(ins):
                count[0] += 1
                ins.then_inc(dve_step, 1)
                dve.wait_ge(dve_step, count[0])

            def moments(src, tiles=range(TILES)):
                for i in tiles:
                    ins = dve.bn_stats(stats[:, i, :], src[:, i, :])
                link(ins)
                for i in tiles:
                    ins = dve.bn_aggr(mv[:, i, :], stats[:, i, :])
                link(ins)
            mean, var = mv[:, :, 0], mv[:, :, 1]

            def ask_root(src, eps, at=slice(0, TILES)):
                count[1] += 1
                dve.tensor_scalar(square[:, at], src, eps, None, ALU.add).then_inc(root_asked, 1)
                return count[1]

            def inverse_root(dst, src, eps):
                number = ask_root(src, eps)
                dve.wait_ge(root_ready, number)
                link(dve.reciprocal(dst[:, :], root[:, :]))

            def minus_mean_times(inv):
                link(dve.scalar_tensor_tensor(out=shift[:, :], in0=mean, scalar=-1.0, in1=inv[:, :],
                                              op0=ALU.mult, op1=ALU.mult))

            def scaled(dst, src, factor, sum_sem=None, tiles=range(TILES), shifts=shift):
                for i in tiles:
                    ins = dve.tensor_scalar(dst[:, i, :], src[:, i, :], factor[:, i:i + 1], shifts[:, i:i + 1],
                                            ALU.mult, ALU.add)
                    if sum_sem is not None and i % QT == QT - 1:
                        ins.then_inc(sum_sem, 1)
                if sum_sem is None:
                    link(ins)

            def times(dst, src, factor):
                for i in range(TILES):
                    ins = dve.tensor_scalar(dst[:, i, :], src[:, i, :], factor[:, i:i + 1], None, ALU.mult)
                    if i % QT == QT - 1:
                        ins.then_inc(rows_ready, 1)

            def norm_of_norm(eps):
                moments(x)
                inverse_root(inv1, var, LN_EPS)
                link(dve.tensor_tensor(scale[:, :], inv1[:, :], inv1[:, :], ALU.mult))
                link(dve.tensor_tensor(scale[:, :], scale[:, :], var, ALU.mult))
                inverse_root(inv2, scale[:, :], eps)

            def add_norm_of_acc():
                moments(acc)
                inverse_root(inv1, var, LN_EPS)
                minus_mean_times(inv1)
                dve.sem_inc(shift_ready, 1)
                first, second = slice(0, TILES // 2), slice(TILES // 2, TILES)
                scaled(acc, acc, inv1, tiles=range(TILES // 2))
                dve.tensor_tensor(x[:, first, :], x[:, first, :], acc[:, first, :], ALU.add)
                dve.wait_ge(acc_normed, 1)
                return dve.tensor_tensor(x[:, second, :], x[:, second, :], acc[:, second, :], ALU.add)

            def attention(ph):
                c = ph.sems

                def rotate(sp_, t, parity, i, x_number, number):
                    queries = t < T_K
                    dve.wait_ge(c["x_bank_empty"], x_number + 1)
                    dve.tensor_tensor(times_sin[0:D1 // 2, i, :], projected[D1 // 2:D1, i, :],
                                      sinT[D1 // 2:D1, :], ALU.mult)
                    dve.tensor_tensor(times_sin[D1 // 2:D1, i, :], projected[0:D1 // 2, i, :],
                                      sinT[0:D1 // 2, :], ALU.mult).then_inc(c["sin_ready"], 1)
                    dve.wait_ge(c["sin_ready"], number + 1)
                    dve.wait_ge(c["cos_ready"], number + 1)
                    if queries and not (isinstance(sp_, int) and sp_ == 0):
                        dve.wait_ge(c["scores_ready"], (sp_ - 1) * ph.units + (t + 1) * ph.group)
                    dst = qT[:, t, :] if queries else kT[:, parity, :]
                    dve.tensor_tensor(dst, times_cos[:, i, :], times_sin[:, i, :], ALU.add)\
                        .then_inc(c["q_ready" if queries else "k_ready"], 1)

                def maximum(s, u):
                    i = u % N_PROB
                    dve.wait_ge(c["scores_ready"], s * ph.units + u + 1)
                    dve.tensor_reduce(negmax[:, i:i + 1], score_bank[u % N_SCORE][:, 0:(Q_ORDER[u % QT] + 1) * P], AX_X,
                                      ALU.max, negate=True).then_inc(c["max_ready"], 1)

                def invert(s, u):
                    i = u % N_PROB
                    dve.wait_ge(c["probs_ready"], PROBS0 + s * ph.units + u + 1)
                    dve.reciprocal(rinv[:, i:i + 1], rowsum[:, i:i + 1]).then_inc(c["rinv_ready"], 1)

                def normalise(s, u):
                    i = u % N_PROB
                    w = (Q_ORDER[u % QT] + 1) * P
                    dve.wait_ge(c["rinv_ready"], s * ph.units + u + 1)
                    dve.tensor_scalar(probs[:, i, 0:w], probs[:, i, 0:w], rinv[:, i:i + 1], None, ALU.mult)\
                        .then_inc(c["norm_ready"], 1)

                def take_values(s, j):
                    dve.wait_ge(c["oT_high_ready"], QTILES * s + j + 1)
                    dve.tensor_tensor(oT_lo[:, j, :], o_bank[:, :], oT_hi[:, j, :].bitcast(F32), ALU.subtract)\
                        .then_inc(c["o_bank_empty"], 1)

                def split_first_keys():
                    dve.wait_ge(c["x_bank_empty"], 1)
                    both_halves = [(kv, slice(kv * D2, (kv + 1) * D2), slice(half * D2, (half + 1) * D2))
                                   for kv in range(2) for half in range(2)]
                    for kv, rows, half in both_halves:
                        ins = dve.tensor_copy(k_hi[half, 0, kv, :], projected[rows, 0, :])
                    ins.then_inc(c["first_high_ready"], 1)
                    dve.wait_ge(c["first_high_ready"], 1)
                    for kv, rows, half in both_halves:
                        ins = dve.tensor_tensor(k_lo[half, 0, kv, :], projected[rows, 0, :],
                                                k_hi[rows, 0, kv, :].bitcast(F32), ALU.subtract)
                    ins.then_inc(c["k_ready"], 1)

                def split_first_queries():
                    dve.wait_ge(c["x_bank_empty"], 2)
                    halves = (slice(0, D2), slice(D2, P))
                    for n in range(2):
                        ins = dve.tensor_copy(q_hl[halves[n], n, :], projected[halves[n], 1, :])
                    ins.then_inc(c["first_high_ready"], 1)
                    dve.wait_ge(c["first_high_ready"], 2)
                    for n in range(2):
                        ins = dve.tensor_tensor(q_hl[halves[1 - n], n, :], projected[halves[n], 1, :],
                                                q_hl[halves[n], n, :].bitcast(F32), ALU.subtract)
                    ins.then_inc(c["q_ready"], 1)

                def add_output(s, i, x_number):
                    dve.wait_ge(c["y_psum_ready"], 2 * s + i + 1)
                    dve.wait_ge(c["x_bank_empty"], x_number)
                    b = s // G
                    dst = acc[:, bass.ds(b * QT + 2 * i, 2), :]
                    dve.tensor_tensor(dst, dst, x_bank[:, :].rearrange("p (i h) -> p i h", i=2), ALU.add)\
                        .then_inc(c["x_bank_empty"], 1)

                for b in range(B):
                    for k in range(KT):
                        dve.wait_ge(hT_high_ready, B * KT * ph.number + KT * b + k + 1)
                        cols = slice(b * S, (b + 1) * S)
                        dve.scalar_tensor_tensor(out=hT_lo[:, k, cols], in0=bank[KT * b + k][:, :],
                                                 scalar=ln_w[:, ph.number, k:k + 1],
                                                 in1=hT_hi[:, k, cols].bitcast(F32),
                                                 op0=ALU.mult, op1=ALU.subtract).then_inc(hT_ready, 1)
                if ph.first:
                    for n, t in enumerate(FIRST_TILES):
                        rotate(0, t, 0, n % 2, n, n)
                else:
                    split_first_keys()
                    split_first_queries()
                    scaled(acc, x, inv1, shifts=norm_shift)
                def slot(s, parity, u, of):
                    back = unit_at(ph, s, u, 2, of)
                    if back:
                        invert(*back)
                    if 0 in of and u < ph.units:
                        maximum(s, u)
                    if back:
                        normalise(*back)
                    for j, d in ph.values_before(u, 2):
                        if d in of:
                            take_values(s + d, j)
                    if ph.first and u >= 1:
                        for e in ph.events(u - 1, "rotate"):
                            if e[2] in of:
                                rotate(s + e[2], e[1], (parity + e[2]) % 2, ph.parity_of(s, parity, e),
                                       ph.number_of(s, e, "x"), ph.number_of(s, e, "rotate"))
                    for e in ph.slots.get(u, []):
                        if e[0] == "output" and e[2] in of:
                            add_output(s + e[2], e[1], ph.number_of(s, e, "x"))
                if ph.first:
                    dve.wait_ge(acc_cleared, 3)
                    dve.wait_ge(rows_cleared, 16 * len(range(0, BLOCKS * SLOTS // P * H, TILES * H)))
                steps(dve, slot, ph)
                dve.wait_ge(c["x_bank_empty"], ph.number_of(STEPS, ("output", 1, -1), "x") + 1)

            dve.wait_ge(x_loaded, 16)
            norm_of_norm(RMS_A_EPS)
            link(dve.tensor_tensor(scale[:, :], inv1[:, :], inv2[:, :], ALU.mult))
            minus_mean_times(scale)
            scaled(htok, x, scale, rows_ready)
            attention(phases[0])

            link(add_norm_of_acc())
            norm_of_norm(RMS_B_EPS)
            link(dve.scalar_tensor_tensor(out=norm_shift[:, :], in0=mean, scalar=-1.0, in1=inv1[:, :],
                                          op0=ALU.mult, op1=ALU.mult))
            link(dve.tensor_tensor(scale[:, :], inv1[:, :], inv2[:, :], ALU.mult))
            minus_mean_times(scale)
            scaled(htok, x, scale, rows_ready)
            attention(phases[1])

            moments(acc)
            link(dve.tensor_tensor(scale[:, :], mean, mean, ALU.mult))
            link(dve.tensor_tensor(scale[:, :], scale[:, :], var, ALU.add))
            inverse_root(inv1, scale[:, :], RMS_B_EPS)
            times(htok, acc, inv1)

            dve.sem_inc(product_ready, PRODUCT0)
            dve.sem_inc(result_ready, RESULT0)
            for par in range(2):
                dve.sem_inc(result_stored[par], 16)
            dve.wait_ge(logits_ready, 1)
            logits = router_bank[:, 0:TILES * E].rearrange("p (i e) -> p i e", e=E)
            link(dve.tensor_copy(pick[:, :, :], logits))
            link(dve.tensor_reduce(e_max[:, :], pick[:, :, :], AX_X, ALU.max))
            link(dve.tensor_tensor(pick[:, :, :], pick[:, :, :],
                                   e_max[:, :].unsqueeze(2).broadcast_to([P, TILES, E]), ALU.subtract))
            dve.sem_inc(e_shifted, 1)
            dve.wait_ge(e_exp_ready, 1)
            link(dve.tensor_reduce(e_sum[:, :], e_prob[:, :, :], AX_X, ALU.add))
            link(dve.reciprocal(e_sum[:, :], e_sum[:, :]))
            link(dve.tensor_tensor(e_prob[:, :, :], e_prob[:, :, :],
                                   e_sum[:, :].unsqueeze(2).broadcast_to([P, TILES, E]), ALU.mult))
            for i in range(TILES):
                ins = dve.max(e_top[:, i, :], e_prob[:, i, :])
            link(ins)
            for i in range(TILES):
                ins = dve.max_index(e_topi[:, i, :], e_top[:, i, :], e_prob[:, i, :])
            link(ins)
            link(dve.tensor_copy(e_topf[:, :, :], e_topi[:, :, :]))
            dve.wait_ge(small_ready, 6)
            for n in range(TOPK):
                ins = dve.tensor_tensor(choice[n][:, :, :], iota_e[:, :, :],
                                        e_topf[:, :, n:n + 1].broadcast_to([P, TILES, E]), ALU.is_equal)
            link(ins)
            dve.tensor_tensor(chosen_b[:, :], choice[0][:, :, :].rearrange("p i e -> p (i e)"),
                              choice[1][:, :, :].rearrange("p i e -> p (i e)"), ALU.add).then_inc(chosen_ready, 1)
            link(dve.tensor_tensor(e_sum[:, :], e_top[:, :, 0], e_top[:, :, 1], ALU.add))
            link(dve.reciprocal(e_sum[:, :], e_sum[:, :]))
            for n in range(TOPK):
                ins = dve.tensor_tensor(share[n][:, :], e_top[:, :, n], e_sum[:, :], ALU.mult)
            link(ins)
            link(dve.memset(run[:, 0, :], 0.0))
            link(dve.memset(first_slot[:, 0:1], 0.0))

            dve.wait_ge(ranks_ready, 1)
            for i in range(TILES):
                link(dve.tensor_tensor(run[:, i + 1, :], run[:, i, :],
                                       router_bank[:, (TILES + i) * E:(TILES + i + 1) * E], ALU.add))
            link(dve.tensor_scalar(whole[:, :], run[:, TILES, :], float(SLOTS - 1), None, ALU.add))
            link(dve.tensor_copy(whole_i[:, :], whole[:, :]))
            link(dve.tensor_scalar(whole_i[:, :], whole_i[:, :], -SLOTS, None, ALU.bitwise_and))
            link(dve.tensor_copy(whole[:, :], whole_i[:, :]))
            for e in range(E):
                link(dve.tensor_tensor(first_slot[:, e + 1:e + 2], first_slot[:, e:e + 1], whole[:, e:e + 1], ALU.add))
            link(dve.tensor_tensor(passed[:, :, :], block_start[:, :, :],
                                   first_slot[:, 1:E + 1].unsqueeze(1).broadcast_to([P, BLOCKS, E]), ALU.is_ge))
            link(dve.tensor_reduce(block_expert_f[:, :], passed[:, :, :], AX_X, ALU.add))
            link(dve.tensor_scalar(block_expert_f[:, :], block_expert_f[:, :], float(E - 1), None, ALU.min))
            dve.tensor_copy(block_expert[:, :], block_expert_f[:, :]).then_inc(experts_ready, 1)
            link(dve.tensor_tensor(place[:, :, :], logits, run[:, 0:TILES, :], ALU.add))
            link(dve.tensor_tensor(place[:, :, :], place[:, :, :],
                                   first_slot[:, 0:E].unsqueeze(1).broadcast_to([P, TILES, E]), ALU.add))
            for n in range(TOPK):
                link(dve.tensor_tensor(pick[:, :, :], place[:, :, :], choice[n][:, :, :], ALU.mult))
                link(dve.tensor_reduce(slot_f[:, :], pick[:, :, :], AX_X, ALU.add))
                ins = dve.tensor_copy(slot_of[n][:, :], slot_f[:, :])
                ins.then_inc(slots_ready, 1)
                dve.wait_ge(slots_ready, n + 1)

            def take_block(j, par):
                dve.wait_ge(block_high_ready, j + 1)
                for k in range(KT):
                    ins = dve.scalar_tensor_tensor(out=slot_lo[:, par, k, :], in0=slot_bank[:, k * SLOTS:(k + 1) * SLOTS],
                                                   scalar=ln_w[:, 2, k:k + 1], in1=slot_hi[:, par, k, :].bitcast(F32),
                                                   op0=ALU.mult, op1=ALU.subtract)
                ins.then_inc(block_T_ready, 1)

            def split_low(j, par, f):
                cols = slice(f * P, (f + 1) * P)
                dve.wait_ge(w13_high_ready, FT * j + f + 1)
                dve.tensor_tensor(w13_lo[:, :, :, cols].rearrange("p n k c -> p (n k) c"),
                                  w13[par][:, :, :, cols].rearrange("p n k c -> p (n k) c"),
                                  w13_hi[:, :, :, cols].rearrange("p n k c -> p (n k) c").bitcast(F32), ALU.subtract)\
                    .then_inc(w13_ready, 1)

            def expert_block(j, par, last=False):
                for f in range(FT + SPLIT_LAG):
                    i, g = f % N_GATED, f - 1
                    if f < FT:
                        dve.wait_ge(relu_ready, FT * j + f + 1)
                        dve.wait_ge(down_done, DOWN0 - N_GATED + FT * j + f + 1)
                        dve.tensor_tensor(gated[:, i, :], up_bank[f % N_UP][:, SLOTS:2 * SLOTS],
                                          rectified[:, f % N_UP, :], ALU.mult).then_inc(product_ready, 1)
                    if 1 <= f <= FT:
                        i = g % N_GATED
                        dve.wait_ge(gated_high_ready, FT * j + g + 1)
                        dve.tensor_tensor(gated_lo[:, i, :], gated[:, i, :], gated_hi[:, i, :].bitcast(F32),
                                          ALU.subtract).then_inc(gated_ready, 1)
                    if f == FT and not last:
                        take_block(j + 1, 1 - par)
                    if f >= SPLIT_LAG and not last:
                        split_low(j + 1, 1 - par, f - SPLIT_LAG)
                dve.wait_ge(down_done, DOWN0 + FT * (j + 1))
                dve.wait_ge(result_stored[par], 16 * (j // 2 + 1))
                dve.tensor_copy(result[:, par, :, :], down_bank[par][:, :].rearrange("p (a h) -> p a h", a=SA))\
                    .then_inc(result_ready, 1)

            for f in range(FT):
                split_low(0, 0, f)
            take_block(0, 0)
            with dve.Fori(0, BLOCKS // 2) as pair:
                for par in range(2):
                    expert_block(2 * pair + par, par)
            expert_block(BLOCKS - 1, 0, True)

            def finish(b, number):
                at = slice(b * QT, (b + 1) * QT)
                dve.wait_ge(root_ready, number)
                link(dve.reciprocal(inv1[:, at], root[:, at]))
                link(dve.scalar_tensor_tensor(out=shift[:, at], in0=mean[:, at], scalar=-1.0, in1=inv1[:, at],
                                              op0=ALU.mult, op1=ALU.mult))
                scaled(acc, acc, inv1, tiles=range(b * QT, (b + 1) * QT))
                dve.tensor_tensor(x[:, at, :], x[:, at, :], acc[:, at, :], ALU.add).then_inc(out_ready, 1)

            asked = []
            for b in range(B):
                tiles = range(b * QT, (b + 1) * QT)
                dve.wait_ge(gathered[b], 16 * TOPK * QT)
                for n, rows in enumerate((htok[:, :, :], hT_rows)):
                    for i in tiles:
                        ins = dve.scalar_tensor_tensor(out=acc[:, i, :], in0=rows[:, i, :], scalar=share[n][:, i:i + 1],
                                                       in1=acc[:, i, :], op0=ALU.mult, op1=ALU.add)
                    link(ins)
                moments(acc, tiles)
                asked.append(ask_root(var[:, b * QT:(b + 1) * QT], LN_EPS, slice(b * QT, (b + 1) * QT)))
                if b:
                    finish(b - 1, asked[b - 1])
            finish(B - 1, asked[B - 1])

        del block


def kernel(**inputs):
    import numpy as np
    import concourse.bacc as bacc
    from concourse.bass_utils import run_bass_kernel_spmd

    a = {k: np.asarray(v) for k, v in inputs.items()}

    def tiles(n, count):
        return a[n].reshape(G, count, H).transpose(0, 2, 1)

    def columns(n, count):
        return a[n].reshape(H, G, count).transpose(1, 0, 2)

    inv_freq = (np.float32(1.0) / np.float32(10000.0) ** (np.arange(0, D1, 2, dtype=np.float32) / np.float32(D1)))
    angle = (np.arange(S, dtype=np.float32)[:, None] * inv_freq.astype(np.float32)).T
    half_scale = float(D1) ** -0.25
    cos, sin = np.cos(angle.astype(np.float64)) * half_scale, np.sin(angle.astype(np.float64)) * half_scale
    arrays = {
        "x_in": a["L0_attn_x"].reshape(T, H),
        "cos_in": np.concatenate([cos, cos]).astype(np.float32),
        "sin_in": np.concatenate([sin, -sin]).astype(np.float32),
        "wa_in": np.concatenate([tiles("L0_attn_q_project", QROWS), tiles("L0_attn_k_project", P),
                                 tiles("L0_attn_v_project", P)], axis=2).reshape(G * H, WROWS),
        "ba_in": np.concatenate([a["L0_attn_q_bias"].reshape(G, QTILES, P), a["L0_attn_k_bias"].reshape(G, 1, P),
                                 a["L0_attn_v_bias"].reshape(G, 1, P)], axis=1).transpose(2, 0, 1),
        "oa_in": a["L0_attn_o_project"].T,
        "wb_in": np.concatenate([columns("L0_ffn_wq", QROWS), columns("L0_ffn_wk", P),
                                 columns("L0_ffn_wv", P)], axis=2).reshape(G * H, WROWS),
        "ob_in": a["L0_ffn_wo"],
        "ln_in": np.stack([a["L0_attn_ln_weight"], a["L0_ffn_ln1_w"], a["L0_ffn_ln2_w"]])
        .reshape(3, KT, P).transpose(2, 0, 1),
        "gate_in": a["L0_ffn_gate_w"],
        "w1_in": a["L0_ffn_w1"].reshape(E * H, F),
        "w2_in": a["L0_ffn_w2"].reshape(E * F, H),
        "w3_in": a["L0_ffn_w3"].reshape(E * H, F),
    }
    arrays = {k: np.ascontiguousarray(v) for k, v in arrays.items()}
    nc = bacc.Bacc("TRN2", target_bir_lowering=False, num_devices=1)
    args = {k: nc.dram_tensor(f"{k}_dram", v.shape, mybir.dt.from_np(v.dtype), kind="ExternalInput").ap()
            for k, v in arrays.items()}
    result = nc.dram_tensor("result_dram", (T, H), F32, kind="ExternalOutput").ap()
    program(nc, out=result, **args)
    r = run_bass_kernel_spmd(nc, [{f"{k}_dram": v for k, v in arrays.items()}], core_ids=[0])
    return r.results[0]["result_dram"].reshape(B, S, H)
```
